# Optimizing a Trainium2 kernel written in Bass

```python
import numpy as np
import jax
import jax.numpy as jnp

def _softmax(x, axis=-1):
    return jax.nn.softmax(x, axis=axis)

def _gelu(x):
    return jax.nn.gelu(x, approximate=True)

def _silu(x):
    return jax.nn.silu(x)

def _sigmoid(x):
    return jax.nn.sigmoid(x)

def _layernorm(x, axis=-1, eps=1e-05):
    m = jnp.mean(x, axis=axis, keepdims=True)
    v = jnp.var(x, axis=axis, keepdims=True)
    return (x - m) / jnp.sqrt(v + eps)

def _scatter_add(tgt, idx, src, axis=0):
    return tgt.at[idx].add(src)

def _segment_sum(src, seg, n):
    return jax.ops.segment_sum(src, seg, n)
kernel_name = 'mk_xattn_seq_d1_seqx_r2_9f31bb'

def setup_inputs(seed: int=0):
    np.random.seed(seed)
    _w = jnp.asarray

    def _rec_inputs():
        import jax
        import jax.numpy as jnp
        _rk = jax.random.key(seed)
        x = -0.0005207 + 1.001 * jax.random.normal(jax.random.fold_in(_rk, 1), (16, 512, 512), jnp.float32)
        _lenS = 512 - jax.random.randint(jax.random.fold_in(_rk, 7), (16,), 0, max(1, 512 // 4) + 1, jnp.int32)
        _lenS2 = 512 - jax.random.randint(jax.random.fold_in(_rk, 8), (16,), 0, max(1, 512 // 4) + 1, jnp.int32)
        _ctx_1024P = jax.random.normal(jax.random.fold_in(_rk, 11), (16, 16, 512), jnp.float32)
        _ctx_1024c = jax.random.dirichlet(jax.random.fold_in(_rk, 511), 0.3 * jnp.ones((16,), jnp.float32), (16, 512))
        _ctx_1024t = jnp.einsum('bsk,bkd->bsd', _ctx_1024c, _ctx_1024P)
        _ctx_1024t = _ctx_1024t * jax.lax.rsqrt(jnp.mean(jnp.square(_ctx_1024t)) + 1e-12) * 0.953939
        ctx_1024 = 4.13588e-05 + 0.999923 * (_ctx_1024t + 0.3 * jax.random.normal(jax.random.fold_in(_rk, 611), (16, 512, 512), jnp.float32))
        return (x, ctx_1024)
    x, ctx_1024 = _rec_inputs()

    def _L0_xattn_setup():
        import jax, jax.numpy as jnp
        import numpy as np
        B, S, R, D, H, FF = (2, 512, 4, 512, 16, 2048)
        HD = D // H
        NEG_INF = jnp.float32(-jnp.inf)

        def _layer_norm(x, g, b, eps=1e-05):
            m = jnp.mean(x, axis=-1, keepdims=True)
            v = jnp.mean((x - m) ** 2, axis=-1, keepdims=True)
            return (x - m) * jax.lax.rsqrt(v + eps) * g + b

        def _forward(query, context, wq, wk, wv, bq, bk, bv, wo, bo, ln1_g, ln1_b, ln2_g, ln2_b, w1, b1, w2, b2):
            Bq, Sq, Dm = query.shape
            Sc = context.shape[1]
            hd = Dm // H
            q = _layer_norm(query, ln1_g, ln1_b)
            qh = (q @ wq + bq).reshape(Bq, Sq, H, hd)
            kh = (context @ wk + bk).reshape(Bq, Sc, H, hd)
            vh = (context @ wv + bv).reshape(Bq, Sc, H, hd)
            scale = 1.0 / jnp.sqrt(jnp.float32(hd))
            scores = jnp.einsum('bqhd,bkhd->bhqk', qh, kh) * scale
            pos_in_block = jnp.arange(Sc) % Sq
            allowed = pos_in_block[None, :] <= jnp.arange(Sq)[:, None]
            scores = jnp.where(allowed[None, None, :, :], scores, NEG_INF)
            probs = jax.nn.softmax(scores, axis=-1)
            o = jnp.einsum('bhqk,bkhd->bqhd', probs, vh).reshape(Bq, Sq, Dm)
            attn_out = o @ wo + bo
            x = query + attn_out
            h = _layer_norm(x, ln2_g, ln2_b)
            ff = jax.nn.gelu(h @ w1 + b1, approximate=False) @ w2 + b2
            return x + ff
        key = jax.random.key(seed)
        ks = jax.random.split(key, 10)
        sc = 0.02
        return {'query': jax.random.normal(ks[0], (B, S, D), dtype=jnp.float32), 'context': jax.random.normal(ks[1], (B, S * R, D), dtype=jnp.float32), 'wq': jax.random.normal(ks[2], (D, D), dtype=jnp.float32) * sc, 'wk': jax.random.normal(ks[3], (D, D), dtype=jnp.float32) * sc, 'wv': jax.random.normal(ks[4], (D, D), dtype=jnp.float32) * sc, 'bq': jnp.zeros((D,), jnp.float32), 'bk': jnp.zeros((D,), jnp.float32), 'bv': jnp.zeros((D,), jnp.float32), 'wo': jax.random.normal(ks[5], (D, D), dtype=jnp.float32) * sc, 'bo': jnp.zeros((D,), jnp.float32), 'ln1_g': jnp.ones((D,), jnp.float32), 'ln1_b': jnp.zeros((D,), jnp.float32), 'ln2_g': jnp.ones((D,), jnp.float32), 'ln2_b': jnp.zeros((D,), jnp.float32), 'w1': jax.random.normal(ks[6], (D, FF), dtype=jnp.float32) * sc, 'b1': jnp.zeros((FF,), jnp.float32), 'w2': jax.random.normal(ks[7], (FF, D), dtype=jnp.float32) * sc, 'b2': jnp.zeros((D,), jnp.float32)}
    _L0_xattn_all = _L0_xattn_setup()
    _L0_xattn_in = {k: v for k, v in _L0_xattn_all.items() if k in ('wq', 'wk', 'wv', 'bq', 'bk', 'bv', 'wo', 'bo', 'ln1_g', 'ln1_b', 'ln2_g', 'ln2_b', 'w1', 'b1', 'w2', 'b2')}
    del _L0_xattn_all
    return {'x': x, 'ctx_1024': ctx_1024, 'L0_xattn_wq': _L0_xattn_in['wq'], 'L0_xattn_wk': _L0_xattn_in['wk'], 'L0_xattn_wv': _L0_xattn_in['wv'], 'L0_xattn_bq': _L0_xattn_in['bq'], 'L0_xattn_bk': _L0_xattn_in['bk'], 'L0_xattn_bv': _L0_xattn_in['bv'], 'L0_xattn_wo': _L0_xattn_in['wo'], 'L0_xattn_bo': _L0_xattn_in['bo'], 'L0_xattn_ln1_g': _L0_xattn_in['ln1_g'], 'L0_xattn_ln1_b': _L0_xattn_in['ln1_b'], 'L0_xattn_ln2_g': _L0_xattn_in['ln2_g'], 'L0_xattn_ln2_b': _L0_xattn_in['ln2_b'], 'L0_xattn_w1': _L0_xattn_in['w1'], 'L0_xattn_b1': _L0_xattn_in['b1'], 'L0_xattn_w2': _L0_xattn_in['w2'], 'L0_xattn_b2': _L0_xattn_in['b2']}

def reference(x, ctx_1024, L0_xattn_wq, L0_xattn_wk, L0_xattn_wv, L0_xattn_bq, L0_xattn_bk, L0_xattn_bv, L0_xattn_wo, L0_xattn_bo, L0_xattn_ln1_g, L0_xattn_ln1_b, L0_xattn_ln2_g, L0_xattn_ln2_b, L0_xattn_w1, L0_xattn_b1, L0_xattn_w2, L0_xattn_b2):
    import jax
    import jax.numpy as jnp

    def _L0_xattn_ref(query, context, wq, wk, wv, bq, bk, bv, wo, bo, ln1_g, ln1_b, ln2_g, ln2_b, w1, b1, w2, b2):
        import jax, jax.numpy as jnp
        import numpy as np
        B, S, R, D, H, FF = (2, 512, 4, 512, 16, 2048)
        HD = D // H
        NEG_INF = jnp.float32(-jnp.inf)

        def _layer_norm(x, g, b, eps=1e-05):
            m = jnp.mean(x, axis=-1, keepdims=True)
            v = jnp.mean((x - m) ** 2, axis=-1, keepdims=True)
            return (x - m) * jax.lax.rsqrt(v + eps) * g + b

        def _forward(query, context, wq, wk, wv, bq, bk, bv, wo, bo, ln1_g, ln1_b, ln2_g, ln2_b, w1, b1, w2, b2):
            Bq, Sq, Dm = query.shape
            Sc = context.shape[1]
            hd = Dm // H
            q = _layer_norm(query, ln1_g, ln1_b)
            qh = (q @ wq + bq).reshape(Bq, Sq, H, hd)
            kh = (context @ wk + bk).reshape(Bq, Sc, H, hd)
            vh = (context @ wv + bv).reshape(Bq, Sc, H, hd)
            scale = 1.0 / jnp.sqrt(jnp.float32(hd))
            scores = jnp.einsum('bqhd,bkhd->bhqk', qh, kh) * scale
            pos_in_block = jnp.arange(Sc) % Sq
            allowed = pos_in_block[None, :] <= jnp.arange(Sq)[:, None]
            scores = jnp.where(allowed[None, None, :, :], scores, NEG_INF)
            probs = jax.nn.softmax(scores, axis=-1)
            o = jnp.einsum('bhqk,bkhd->bqhd', probs, vh).reshape(Bq, Sq, Dm)
            attn_out = o @ wo + bo
            x = query + attn_out
            h = _layer_norm(x, ln2_g, ln2_b)
            ff = jax.nn.gelu(h @ w1 + b1, approximate=False) @ w2 + b2
            return x + ff
        return _forward(query, context, wq, wk, wv, bq, bk, bv, wo, bo, ln1_g, ln1_b, ln2_g, ln2_b, w1, b1, w2, b2)
    x = _L0_xattn_ref(x, ctx_1024, L0_xattn_wq, L0_xattn_wk, L0_xattn_wv, L0_xattn_bq, L0_xattn_bk, L0_xattn_bv, L0_xattn_wo, L0_xattn_bo, L0_xattn_ln1_g, L0_xattn_ln1_b, L0_xattn_ln2_g, L0_xattn_ln2_b, L0_xattn_w1, L0_xattn_b1, L0_xattn_w2, L0_xattn_b2)
    return x

_drawn_inputs = setup_inputs


def setup_inputs(seed=0):
    import zlib

    import numpy as np

    out = dict(_drawn_inputs(seed))
    spreads = {'L0_xattn_bq': (0.0, 0.8),
     'L0_xattn_bk': (0.0, 0.8),
     'L0_xattn_bv': (0.0, 0.1),
     'L0_xattn_bo': (0.0, 0.1),
     'L0_xattn_ln1_g': (1.0, 0.6),
     'L0_xattn_ln1_b': (0.0, 0.8),
     'L0_xattn_ln2_g': (1.0, 0.2),
     'L0_xattn_ln2_b': (0.0, 0.341),
     'L0_xattn_b1': (0.0, 0.1),
     'L0_xattn_b2': (0.0, 0.1)}
    factors = {'L0_xattn_wq': 6.985, 'L0_xattn_wk': 6.837}
    for name, (base, spread) in spreads.items():
        noise = np.random.default_rng([zlib.crc32(name.encode()), seed]).standard_normal(out[name].shape)
        drawn = base * np.exp(spread * noise) if base else spread * noise
        out[name] = jnp.asarray(drawn.astype(out[name].dtype))
    for name, factor in factors.items():
        out[name] = (out[name] * factor).astype(out[name].dtype)
    return out
```

```python
from contextlib import ExitStack

import concourse.bass as bass
from concourse import mybir
from concourse.alu_op_type import AluOpType as ALU

ACT = mybir.ActivationFunctionType
F32 = mybir.dt.float32
F32R = mybir.dt.float32r
BF16 = mybir.dt.bfloat16

P = 128
EPS = 1e-5
MASKED = 3.0e38

HEADS = 16
RING_S = 3
POS = [0, 1, 3, 2]


def tile_of(k):
    if k < 4:
        return 0, k, (0, 1)
    return 1, (k - 4) // 2, (2 + (k - 4) % 2,)


def act_moves(k):
    return k >= 4 and (k - 4) % 2 == 1


def stage_a(nc, x, ctxT, wq, wk, wv, wo, vecs, bo, x1):
    B, S, D = x.shape
    HD = D // HEADS
    KT = D // P
    QT = S // P
    NG = HEADS // 4
    TG = 12
    TB = NG * TG
    SCALE = float(HD) ** -0.5

    PRO = ["X0", "X1", "X2", "X3", "Q0", "K0", "V0", "V1", "V2", "V3"]
    LOOP = ["Q1", "K1", "Q2", "R0", "K2", "Q3", "R1", "K3", "X0", "X1", "X2", "R2", "X3", "Q0", "K0",
            "V0", "V1", "R3", "V2", "V3", "O0", "O1", "O2", "O3"]
    LAST = ["Q1", "K1", "Q2", "R0", "K2", "Q3", "R1", "K3", "R2", "R3", "O0", "O1", "O2", "O3"]
    assert len(PRO) % 2 == 0 and len(LOOP) % 2 == 0

    with ExitStack() as ctx:
        def sb(name, shape, dt=F32):
            return ctx.enter_context(nc.sbuf_tensor(name, shape, dt))

        def pb(name):
            return ctx.enter_context(nc.psum_tensor(name, [P, 512], F32))

        def sem(name):
            return ctx.enter_context(nc.semaphore(name))

        w_hi = [sb(f"{n}_hi", [P, KT, D], F32R) for n in ("wq", "wk", "wv", "wo")]
        w_lo = [sb(f"{n}_lo", [P, KT, D], F32R) for n in ("wq", "wk", "wv", "wo")]
        vec = sb("vec", [P, 5, 4])
        bqs = sb("bqs", [P, NG])
        bo_row = sb("bo_row", [P, D])
        xt = sb("xt", [P, QT, D])
        xnT_hi = sb("xnT_hi", [P, KT, S], F32R)
        xnT_lo = sb("xnT_lo", [P, KT, S], F32R)
        c_raw = sb("c_raw", [P, 2, S])
        cT_hi = sb("cT_hi", [P, KT, S], F32R)
        cT_lo = sb("cT_lo", [P, KT, S], F32R)
        st_hi = sb("st_hi", [P, 2, S], F32R)
        st_lo = sb("st_lo", [P, 2, S], F32R)
        stack = sb("stack", [P, 2, 2, 4, S], F32R)
        v_sb = sb("v_sb", [P, QT, D])
        sm = sb("sm", [P, RING_S, 512])
        pT = sb("pT", [P, 4, 1280])
        rT = sb("rT", [P, 512])
        rexp = sb("rexp", [P, 4, 4, HD])
        oT_hi = sb("oT_hi", [P, NG, S], F32R)
        oT_lo = sb("oT_lo", [P, NG, S], F32R)
        mask = sb("mask", [P, 512], BF16)
        ident = sb("ident", [P, P])
        mins = sb("mins", [P, 2, 16])
        sums = sb("sums", [P, 2, 16])
        recips = sb("recips", [P, 2, 16])
        stats = sb("stats", [P, QT, 6])
        mv = sb("mv", [P, QT, 2])
        ve = sb("ve", [P, QT])
        rstd = sb("rstd", [P, QT])
        nhalf = sb("nhalf", [P, QT])
        raw = pT[:].rearrange("p a b -> p (a b)")
        bvx = sm[:, 0, :].rearrange("p (t m) -> p t m", t=KT)

        bank_s = [pb(f"bank_s{i}") for i in range(RING_S)]
        bank_t = [pb(f"bank_t{i}") for i in range(2)]
        bank_v = pb("bank_v")
        bank_d = [pb(f"bank_d{i}") for i in range(2)]

        vec_in, bo_in = sem("vec_in"), sem("bo_in")
        raw_in = [sem(f"raw_in{i}") for i in range(4)]
        x_in, res_in, stored = sem("x_in"), sem("res_in"), sem("stored")
        c_in = [sem(f"c_in{i}") for i in range(2)]
        stacked = sem("stacked")
        carriers = sem("carriers")
        ready = sem("ready")
        consts, bias_mm, scaled, w_hi_done, w_lo_done, bvx_ok, bias_ok = (
            sem(n) for n in ("consts", "bias_mm", "scaled", "w_hi_done", "w_lo_done", "bvx_ok", "bias_ok"))
        scored, masked, probs, transposed, pv_done = (
            sem(n) for n in ("scored", "masked", "probs", "transposed", "pv_done"))
        moved = [sem(f"moved{i}") for i in range(2)]
        recip_ok, rexp_ok, o_prod, oT_hi_ok, oT_done = (
            sem(n) for n in ("recip_ok", "rexp_ok", "o_prod", "oT_hi_ok", "oT_done"))
        dense = sem("dense")
        d_free = [sem(f"d_free{i}") for i in range(2)]
        qk_hi, x_hi = sem("qk_hi"), sem("x_hi")
        bn_ok, mv_ok, ve_ok, rstd_ok, xn_ok, c_hi_ok, c_done, res_ok = (
            sem(n) for n in ("bn_ok", "mv_ok", "ve_ok", "rstd_ok", "xn_ok", "c_hi_ok", "c_done", "res_ok"))

        def bank_wait(n):
            return n // 2 + 1

        def bank_read(n):
            return n // 2 + 2

        class Iteration:
            def __init__(self, b, last):
                self.b, self.last = b, last
                self.names = LAST if last else LOOP
            def job(self, name):
                return self.names.index(name)
            def bank(self, name):
                return self.job(name) % 2
            def done(self, name):
                return self.b * len(LOOP) + (len(PRO) + self.job(name) + 1)
            def bank_wait(self, name):
                return self.b * (len(LOOP) // 2) + bank_wait(len(PRO) + self.job(name))
            def bank_read(self, name):
                return self.b * (len(LOOP) // 2) + bank_read(len(PRO) + self.job(name))

        class Prologue:
            b, last = -1, False
            def job(self, name):
                return PRO.index(name)
            def bank(self, name):
                return self.job(name) % 2
            def done(self, name):
                return self.job(name) + 1
            def bank_wait(self, name):
                return bank_wait(self.job(name))
            def bank_read(self, name):
                return bank_read(self.job(name))

        def over_batches(eng, body):
            if B > 1:
                with eng.Fori(0, B - 1) as b:
                    body(Iteration(b, False))
            body(Iteration(B - 1, True))

        def qk_jobs(it, g):
            if g < NG - 1:
                return f"Q{g + 1}", f"K{g + 1}", it.b * NG + (g + 1)
            return "Q0", "K0", it.b * NG + NG

        x_v = x.rearrange("b (t p) d -> b p t d", p=P)
        x1_v = x1.rearrange("b (t p) d -> b p t d", p=P)
        c_v = ctxT.rearrange("b (t p) s -> b p t s", p=P)

        block = ctx.enter_context(nc.Block())

        @block.sync
        def _(sp):
            def one(view, b):
                return view[bass.ds(b, 1)].rearrange("o p t d -> p (o t) d")

            def load_c(m, fb):
                sp.dma_start(c_raw[:, fb % 2, :], one(c_v, m)[:, fb, :]).then_inc(c_in[fb % 2], 16)

            def stack_parts(it, w, job, par):
                sp.wait_ge(d_free[it.bank(job)], it.bank_read(job))
                for part, src in enumerate(((st_hi, st_hi, st_lo, st_lo), (st_hi, st_lo, st_hi, st_lo))[w]):
                    sp.dma_start(stack[32 * part:32 * part + 32, par, w, :, :].bitcast(F32),
                                 src[:, w, :].bitcast(F32)).then_inc(stacked, 16)

            sp.sem_inc(stored, 16)
            sp.dma_start(vec[:], vecs).then_inc(vec_in, 16)
            sp.dma_start(xt[:], one(x_v, 0)).then_inc(x_in, 16)
            sp.dma_start(bo_row[:], bo.partition_broadcast(P)).then_inc(bo_in, 16)
            for i, w in enumerate((wq, wk)):
                sp.dma_start(raw[:, 2048 * i:2048 * i + 2048].rearrange("p (t n) -> p t n", t=KT),
                             w.rearrange("(t p) n -> p t n", p=P)).then_inc(raw_in[i], 16)
            load_c(0, 0)
            load_c(0, 1)
            for i, w in enumerate((wv, wo)):
                sp.wait_ge(w_lo_done, i + 1)
                sp.dma_start(raw[:, 2048 * i:2048 * i + 2048].rearrange("p (t n) -> p t n", t=KT),
                             w.rearrange("(t p) n -> p t n", p=P)).then_inc(raw_in[i + 2], 16)
                sp.wait_ge(c_done, i + 1)
                load_c(0, 2 + i)
            for w, job in enumerate(("Q0", "K0")):
                stack_parts(Prologue(), w, job, 0)

            def body(it):
                b = it.b
                if not it.last:
                    sp.wait_ge(stored, b * 64 + 16)
                    sp.dma_start(xt[:], one(x_v, b + 1)).then_inc(x_in, 16)
                    sp.wait_ge(c_done, b * 4 + 4)
                    load_c(b + 1, 0)
                    load_c(b + 1, 1)
                for g in range(NG):
                    if g == NG - 1:
                        if it.last:
                            sp.wait_ge(stored, b * 64 + 16)
                        else:
                            for fb in (2, 3):
                                sp.wait_ge(c_done, b * 4 + (3 + fb))
                                load_c(b + 1, fb)
                            sp.wait_ge(dense, it.done("X3"))
                        sp.dma_start(xt[:], one(x_v, b)).then_inc(res_in, 16)
                        if it.last:
                            continue
                    qj, kj, _ = qk_jobs(it, g)
                    if g > 0:
                        sp.wait_ge(scored, b * TB + TG * g)
                        sp.sem_inc(carriers, 1)
                    else:
                        sp.wait_ge(scored, b * TB + 1)
                        sp.sem_inc(carriers, 1)
                    for w, job in ((0, qj), (1, kj)):
                        stack_parts(it, w, job, (g + 1) % 2)
                for t in range(QT):
                    sp.wait_ge(d_free[it.bank(f"O{t}")], it.bank_read(f"O{t}"))
                    sp.dma_start(one(x1_v, b)[:, t, :], xt[:, t, :]).then_inc(stored, 16)

            over_batches(sp, body)
            sp.wait_ge(stored, 64 * B + 16)

        @block.tensor
        def _(pe):
            def split_product(out, lh, ll, rh, rl, first, last):
                pe.matmul(out, lh, rh, start=first, stop=False)
                pe.matmul(out, lh, rl, start=False, stop=False)
                return pe.matmul(out, ll, rh, start=False, stop=last)

            def x_transpose(it, t, m):
                job = f"X{t}"
                pe.wait_ge(xn_ok, m * QT + (t + 1))
                pe.wait_ge(d_free[it.bank(job)], it.bank_wait(job))
                for f in range(KT):
                    mm = pe.transpose(bank_d[it.bank(job)][:, P * f:P * f + P], xt[:, t, P * f:P * f + P], ident[:])
                mm.then_inc(dense, 1)

            def qk_product(it, w, job, g, kts):
                bank = bank_d[it.bank(job)]
                hi, lo = ((xnT_hi, xnT_lo), (cT_hi, cT_lo))[w]
                if kts[0] == 0:
                    pe.wait_ge(d_free[it.bank(job)], it.bank_wait(job))
                for kt in kts:
                    cols = slice(P * g, P * g + P)
                    mm = split_product(bank[:], w_hi[w][:, kt, cols], w_lo[w][:, kt, cols],
                                       hi[:, kt, :], lo[:, kt, :], kt == 0, kt == KT - 1)
                if kts[-1] == KT - 1:
                    mm.then_inc(dense, 1)

            def v_product(it, t):
                job = f"V{t}"
                pe.wait_ge(d_free[it.bank(job)], it.bank_wait(job))
                for kt in range(KT):
                    cols = slice(P * t, P * t + P)
                    mm = split_product(bank_d[it.bank(job)][:], cT_hi[:, kt, cols], cT_lo[:, kt, cols],
                                       w_hi[2][:, kt, :], w_lo[2][:, kt, :], kt == 0, kt == KT - 1)
                mm.then_inc(dense, 1)

            def o_product(it, t):
                job = f"O{t}"
                if t == 0:
                    pe.wait_ge(oT_done, it.b * NG + (NG + 1))
                pe.wait_ge(d_free[it.bank(job)], it.bank_wait(job))
                for g in range(NG):
                    cols = slice(P * POS[t], P * POS[t] + P)
                    mm = split_product(bank_d[it.bank(job)][:], oT_hi[:, g, cols], oT_lo[:, g, cols],
                                       w_hi[3][:, g, :], w_lo[3][:, g, :], g == 0, g == NG - 1)
                mm.then_inc(dense, 1)

            def score(it, n):
                g, k = divmod(n, TG)
                _, r, qts = tile_of(k)
                if k == 0:
                    pe.wait_ge(stacked, it.b * (128 * NG) + 128 * (g + 1))
                pe.wait_ge(masked, it.b * TB + (n + 1))
                off = 0
                for qt in qts:
                    w = P * (qt + 1)
                    mm = pe.matmul(bank_s[n % RING_S][:, off:off + w], stack[:, g % 2, 0, r, P * qt:P * qt + P],
                                   stack[:, g % 2, 1, r, 0:w], start=True, stop=True)
                    off += w
                mm.then_inc(scored, 1)

            def p_transpose(it, n):
                k = n % TG
                _, r, qts = tile_of(k)
                pe.wait_ge(probs, it.b * TB + (n + 1))
                pe.wait_ge(moved[n % 2], it.b * (TB // 2) + (n // 2 + 1))
                for c in range(sum(qt + 1 for qt in qts)):
                    mm = pe.transpose(bank_t[n % 2][:, P * c:P * c + P], sm[:, n % RING_S, P * c:P * c + P], ident[:])
                mm.then_inc(transposed, 1)

            def pv(it, g, pair):
                last_tile = TG * g + (3 if pair == 0 else 11)
                for i in range(2):
                    pe.wait_ge(moved[i], it.b * (TB // 2) + ((last_tile + 1) // 2 + 1))
                if pair == 0:
                    pe.wait_ge(o_prod, it.b * NG + (g + 1))
                    if g == 0:
                        for name in ("V2", "V3"):
                            pro = Prologue()
                            pe.wait_ge(d_free[pro.bank(name)], it.b * (len(LOOP) // 2) + pro.bank_read(name))
                    parts = [(0, 0, 256, 0), (1, 256, 128, 128)]
                else:
                    parts = [(0, 384, 256, 256), (1, 640, 256, 256), (2, 896, 256, 256), (3, 1152, 128, 256)]
                for j, at, w, to in parts:
                    for r in range(4):
                        h = 4 * g + r
                        mm = pe.matmul(bank_v[32 * r:32 * r + 32, to:to + w], v_sb[:, j, HD * h:HD * h + HD],
                                       pT[:, r, at:at + w], start=(j == 0), stop=(j == len(parts) - 1),
                                       skip_group_check=True)
                mm.then_inc(pv_done, 1)

            def r_transpose(it, g):
                job = f"R{g}"
                pe.wait_ge(rexp_ok, it.b * NG + (g + 1))
                pe.wait_ge(d_free[it.bank(job)], it.bank_wait(job))
                for c in range(QT):
                    mm = pe.transpose(bank_d[it.bank(job)][:, P * c:P * c + P],
                                      rexp[:, c, :, :].rearrange("p a b -> p (a b)"), ident[:])
                mm.then_inc(dense, 1)

            pe.sem_inc(transposed, 3)
            pe.sem_inc(pv_done, 2)
            pe.wait_ge(vec_in, 16)
            pe.wait_ge(raw_in[0], 16)
            for g in range(NG):
                for kt in range(KT):
                    mm = pe.matmul(bank_s[0][:, g:g + 1], raw[:, D * kt + P * g:D * kt + P * g + P],
                                   vec[:, 1, kt:kt + 1], start=(kt == 0), stop=(kt == KT - 1))
            mm.then_inc(bias_mm, 1)
            pro = Prologue()
            pe.wait_ge(consts, 1)
            for t in range(QT):
                x_transpose(pro, t, 0)
            pe.wait_ge(w_lo_done, 1)
            pe.wait_ge(d_free[1], pro.bank_read("X3"))
            pe.wait_ge(d_free[0], pro.bank_read("X2"))
            qk_product(pro, 0, "Q0", 0, range(KT))
            pe.wait_ge(w_lo_done, 2)
            pe.wait_ge(c_done, 4)
            qk_product(pro, 1, "K0", 0, range(KT))
            pe.wait_ge(w_lo_done, 3)
            for t in range(QT):
                v_product(pro, t)
            pe.wait_ge(bvx_ok, 1)
            pe.wait_ge(raw_in[3], 16)
            for kt in range(KT):
                mm = pe.matmul(bank_s[1][:], bvx[:, kt, :], raw[:, 2048 + D * kt:2048 + D * kt + D],
                               start=(kt == 0), stop=(kt == KT - 1))
            mm.then_inc(bias_mm, 1)
            pe.wait_ge(w_lo_done, 4)
            pe.wait_ge(bias_ok, 2)

            def body(it):
                for n in range(TB + 2):
                    g, k = divmod(n, TG)
                    if n < TB:
                        score(it, n)
                    if n >= 2:
                        p_transpose(it, n - 2)
                    if g < NG:
                        if k == 7:
                            pv(it, g, 0)
                        if g > 0 and k == 3:
                            pv(it, g - 1, 1)
                            r_transpose(it, g - 1)
                        if g < NG - 1:
                            qj, kj, _ = qk_jobs(it, g)
                            if k < 3:
                                qk_product(it, 0, qj, g + 1, ((0,), (1,), (2, 3))[k])
                            if 4 <= k < 7:
                                qk_product(it, 1, kj, g + 1, ((0,), (1,), (2, 3))[k - 4])
                        elif not it.last:
                            if k in (0, 1, 2, 4):
                                x_transpose(it, (0, 1, 2, None, 3)[k], it.b + 1)
                            if k == 6:
                                for i in range(2):
                                    name = ("X2", "X3")[i]
                                    pe.wait_ge(d_free[it.bank(name)], it.bank_read(name))
                            if 6 <= k < 9:
                                qk_product(it, 0, "Q0", 0, ((0,), (1,), (2, 3))[k - 6])
                            if k == 9:
                                pe.wait_ge(c_done, it.b * 4 + 8)
                            if 9 <= k < 12:
                                qk_product(it, 1, "K0", 0, ((0,), (1,), (2, 3))[k - 9])
                if not it.last:
                    v_product(it, 0)
                pv(it, NG - 1, 1)
                if not it.last:
                    v_product(it, 1)
                r_transpose(it, NG - 1)
                if not it.last:
                    v_product(it, 2)
                    v_product(it, 3)
                for t in range(QT):
                    o_product(it, t)

            over_batches(pe, body)

        def move_tile(eng, copy, it, n):
            g, k = divmod(n, TG)
            pair, r, qts = tile_of(k)
            eng.wait_ge(transposed, it.b * TB + (n + 4))
            eng.wait_ge(pv_done, it.b * (2 * NG) + (2 * g + pair + 1))
            bank = bank_t[n % 2]
            if pair == 0:
                out, src = pT[:, r, 0:384], bank[:, 0:384]
            else:
                qt = qts[0]
                first = 0 if qt == 3 else P
                out = pT[:, r, 384:1280].rearrange("p (c q) -> p c q", q=P)[:, first // P::2, :]
                src = bank[:, 0:P * (qt + 1)].rearrange("p (c q) -> p c q", q=P)
            copy(out, src).then_inc(moved[n % 2], 1)

        @block.vector
        def _(dve):
            V = nc.vector

            def layer_norm_stats(m):
                dve.wait_ge(x_in, m * 16 + 16)
                for t in range(QT):
                    V.bn_stats(stats[:, t, :], xt[:, t, :]).then_inc(bn_ok, 1)
                for t in range(QT):
                    dve.wait_ge(bn_ok, m * QT + (t + 1))
                    dve.sem_inc(carriers, 1)
                    V.bn_aggr(mv[:, t, :], stats[:, t, :]).then_inc(mv_ok, 1)
                dve.wait_ge(mv_ok, m * QT + QT)
                V.tensor_scalar(ve[:], mv[:, :, 1], EPS, None, ALU.add).then_inc(ve_ok, 1)

            def normalise(m, t):
                if t == 0:
                    dve.wait_ge(rstd_ok, m + 1)
                V.tensor_scalar(xt[:, t, :], xt[:, t, :], mv[:, t, 0:1], rstd[:, t:t + 1],
                                ALU.subtract, ALU.mult).then_inc(xn_ok, 1)

            def x_low(it, t, m):
                job = f"X{t}"
                dve.wait_ge(x_hi, m * QT + (t + 1))
                cols = slice(P * t, P * t + P)
                V.tensor_tensor(xnT_lo[:, :, cols], bank_d[it.bank(job)][:].rearrange("p (f c) -> p f c", f=KT),
                                xnT_hi[:, :, cols].bitcast(F32), ALU.subtract).then_inc(d_free[it.bank(job)], 1)

            def qk_low(it, w, job, g, G):
                dve.wait_ge(qk_hi, G * 2 + (w + 1))
                bias = bqs[:, g:g + 1] if w == 0 else vec[:, 3, g:g + 1]
                V.scalar_tensor_tensor(st_lo[:, w, :], bank_d[it.bank(job)][:], bias, st_hi[:, w, :].bitcast(F32),
                                       ALU.add, ALU.subtract).then_inc(d_free[it.bank(job)], 1)

            def mask_and_max(it, n):
                g, k = divmod(n, TG)
                _, r, qts = tile_of(k)
                dve.wait_ge(scored, it.b * TB + (n + 1))
                dve.wait_ge(transposed, it.b * TB + (n + 1))
                dve.sem_inc(carriers, 1)
                off = 0
                for qt in qts:
                    w = P * (qt + 1)
                    c = 4 * POS[qt] + r
                    op = V.tensor_tensor_reduce(sm[:, n % RING_S, off:off + w], bank_s[n % RING_S][:, off:off + w],
                                                mask[:, 512 - w:512], 1.0, 0.0, ALU.add, ALU.min,
                                                mins[:, g % 2, c:c + 1])
                    off += w
                op.then_inc(masked, 1)

            def o_product(it, g):
                job = f"R{g}"
                dve.wait_ge(d_free[it.bank(job)], it.bank_read(job))
                dve.wait_ge(pv_done, it.b * (2 * NG) + (2 * g + 4))
                V.tensor_tensor(rT[:], bank_v[:], rT[:], ALU.mult).then_inc(o_prod, 1)

            dve.sem_inc(masked, 3)
            dve.sem_inc(o_prod, 1)
            for i in range(2):
                dve.sem_inc(moved[i], 1)
                dve.sem_inc(d_free[i], 1)
            dve.wait_ge(vec_in, 16)
            V.tensor_copy(bvx, vec[:, 4, :].unsqueeze(2).to_broadcast([P, KT, P])).then_inc(bvx_ok, 1)
            layer_norm_stats(0)
            dve.wait_ge(bias_mm, 1)
            V.tensor_tensor(bqs[:], bank_s[0][:, 0:NG], vec[:, 2, :], ALU.add).then_inc(bias_ok, 1)
            for t in range(QT):
                normalise(0, t)
            dve.wait_ge(raw_in[0], 16)
            for kt in range(KT):
                V.tensor_scalar(raw[:, D * kt:D * kt + D], raw[:, D * kt:D * kt + D], vec[:, 0, kt:kt + 1], -SCALE,
                                ALU.mult, ALU.mult).then_inc(scaled, 1)
            dve.wait_ge(bias_ok, 1)
            V.tensor_scalar(bqs[:], bqs[:], -SCALE, None, ALU.mult).then_inc(scaled, 1)
            for i in range(4):
                dve.wait_ge(w_hi_done, i + 1)
                at = 2048 * (i % 2)
                V.tensor_tensor(w_lo[i][:].rearrange("p t n -> p (t n)"), raw[:, at:at + 2048],
                                w_hi[i][:].rearrange("p t n -> p (t n)").bitcast(F32),
                                ALU.subtract).then_inc(w_lo_done, 1)
                if i == 0:
                    for t in range(QT):
                        x_low(Prologue(), t, 0)
                    dve.wait_ge(scaled, KT + 1)
                    qk_low(Prologue(), 0, "Q0", 0, 0)
            qk_low(Prologue(), 1, "K0", 0, 0)
            dve.wait_ge(bias_mm, 2)
            dve.wait_ge(bo_in, 16)
            V.tensor_tensor(bo_row[:], bank_s[1][:], bo_row[:], ALU.add).then_inc(bias_ok, 1)
            dve.wait_ge(consts, 2)

            def body(it):
                for n in range(TB + 3):
                    g, k = divmod(n, TG)
                    if n < TB:
                        mask_and_max(it, n)
                    if n >= 3 and not act_moves((n - 3) % TG):
                        move_tile(dve, V.tensor_copy, it, n - 3)
                    if g > 0 and k == 1:
                        dve.wait_ge(probs, it.b * TB + TG * g)
                        V.reciprocal(recips[:, (g - 1) % 2, :], sums[:, (g - 1) % 2, :]).then_inc(recip_ok, 1)
                    if g < NG:
                        if g > 0 and k == 5:
                            o_product(it, g - 1)
                        if g < NG - 1:
                            qj, kj, G = qk_jobs(it, g)
                            if k == 3:
                                qk_low(it, 0, qj, g + 1, G)
                            if k == 7:
                                qk_low(it, 1, kj, g + 1, G)
                            if g == 1 and k == 9 and not it.last:
                                layer_norm_stats(it.b + 1)
                            if g == 2 and k in (8, 9, 10, 11) and not it.last:
                                normalise(it.b + 1, k - 8)
                        elif not it.last:
                            if k in (1, 2, 3, 5):
                                x_low(it, (None, 0, 1, 2, None, 3)[k], it.b + 1)
                            if k == 9:
                                qk_low(it, 0, "Q0", 0, qk_jobs(it, g)[2])
                if not it.last:
                    qk_low(it, 1, "K0", 0, qk_jobs(it, NG - 1)[2])
                o_product(it, NG - 1)
                for t in range(QT):
                    job = f"O{t}"
                    dve.wait_ge(dense, it.done(job))
                    dve.wait_ge(res_ok, it.b * QT + (t + 1))
                    V.tensor_tensor(xt[:, t, :], bank_d[it.bank(job)][:], xt[:, t, :],
                                    ALU.add).then_inc(d_free[it.bank(job)], 1)

            over_batches(dve, body)

        @block.scalar
        def _(act):
            A = nc.scalar

            def x_high(it, t, m):
                job = f"X{t}"
                act.wait_ge(dense, it.done(job))
                A.copy(xnT_hi[:, :, P * t:P * t + P],
                       bank_d[it.bank(job)][:].rearrange("p (f c) -> p f c", f=KT)).then_inc(x_hi, 1)

            def qk_high(it, w, job, g, G):
                act.wait_ge(dense, it.done(job))
                if not isinstance(G, int) or G > 0:
                    act.wait_ge(stacked, G * 128)
                bias = bqs[:, g:g + 1] if w == 0 else vec[:, 3, g:g + 1]
                A.activation(st_hi[:, w, :], bank_d[it.bank(job)][:], ACT.Identity, bias=bias,
                             scale=1.0).then_inc(qk_hi, 1)

            def v_copy(it, t, pv_count):
                job = f"V{t}"
                act.wait_ge(dense, it.done(job))
                act.wait_ge(pv_done, pv_count)
                A.copy(v_sb[:, t, :], bank_d[it.bank(job)][:]).then_inc(d_free[it.bank(job)], 1)

            def exponential(it, n):
                g, k = divmod(n, TG)
                _, r, qts = tile_of(k)
                act.wait_ge(masked, it.b * TB + (n + 4))
                off = 0
                for qt in qts:
                    w = P * (qt + 1)
                    c = 4 * POS[qt] + r
                    row = sm[:, n % RING_S, off:off + w]
                    op = A.activation(row, row, ACT.Exp, bias=mins[:, g % 2, c:c + 1], scale=-1.0,
                                      accum_out=sums[:, g % 2, c:c + 1])
                    off += w
                op.then_inc(probs, 1)

            def r_copy(it, g):
                job = f"R{g}"
                act.wait_ge(dense, it.done(job))
                act.wait_ge(oT_done, it.b * NG + (g + 1))
                A.copy(rT[:], bank_d[it.bank(job)][:]).then_inc(d_free[it.bank(job)], 1)

            def o_high(it, g):
                act.wait_ge(o_prod, it.b * NG + (g + 2))
                act.wait_ge(dense, it.done("Q1"))
                A.copy(oT_hi[:, g, :], rT[:]).then_inc(oT_hi_ok, 1)

            for i in range(4):
                act.wait_ge(raw_in[i], 16)
                if i == 0:
                    act.wait_ge(scaled, KT)
                at = 2048 * (i % 2)
                A.copy(w_hi[i][:].rearrange("p t n -> p (t n)"), raw[:, at:at + 2048]).then_inc(w_hi_done, 1)
                if i == 0:
                    for t in range(QT):
                        x_high(Prologue(), t, 0)
                    act.wait_ge(scaled, KT + 1)
                    qk_high(Prologue(), 0, "Q0", 0, 0)
            qk_high(Prologue(), 1, "K0", 0, 0)
            for t in range(QT):
                v_copy(Prologue(), t, 2)

            def body(it):
                for n in range(TB + 3):
                    g, k = divmod(n, TG)
                    if n < TB:
                        exponential(it, n)
                    if n >= 3 and act_moves((n - 3) % TG):
                        move_tile(act, A.copy, it, n - 3)
                    if g < NG:
                        if g > 0 and k == 4:
                            r_copy(it, g - 1)
                        if g > 0 and k == 6:
                            o_high(it, g - 1)
                        if g < NG - 1:
                            qj, kj, G = qk_jobs(it, g)
                            if k == 3:
                                qk_high(it, 0, qj, g + 1, G)
                            if k == 7:
                                qk_high(it, 1, kj, g + 1, G)
                        elif not it.last:
                            if k in (1, 2, 3, 5):
                                x_high(it, (None, 0, 1, 2, None, 3)[k], it.b + 1)
                            if k == 9:
                                qk_high(it, 0, "Q0", 0, qk_jobs(it, g)[2])
                pv_count = it.b * (2 * NG) + (2 * NG + 2)
                if not it.last:
                    qk_high(it, 1, "K0", 0, qk_jobs(it, NG - 1)[2])
                    v_copy(it, 0, pv_count)
                    v_copy(it, 1, pv_count)
                r_copy(it, NG - 1)
                if not it.last:
                    v_copy(it, 2, pv_count)
                o_high(it, NG - 1)
                if not it.last:
                    v_copy(it, 3, pv_count)

            over_batches(act, body)

        @block.gpsimd
        def _(pool):
            G_ = nc.gpsimd

            def split_context(m, fb):
                pool.wait_ge(c_in[fb % 2], m * 32 + 16 * (fb // 2 + 1))
                pool.sem_inc(carriers, 1)
                G_.tensor_copy(cT_hi[:, fb, :], c_raw[:, fb % 2, :]).then_inc(c_hi_ok, 1)
                pool.wait_ge(c_hi_ok, m * 4 + (fb + 1))
                G_.tensor_tensor(out=cT_lo[:, fb, :], in0=c_raw[:, fb % 2, :], in1=cT_hi[:, fb, :].bitcast(F32),
                                 op=ALU.subtract).then_inc(c_done, 1)

            def inverse_root(m):
                pool.wait_ge(ve_ok, m + 1)
                G_.tensor_tensor(out=rstd[:], in0=ve[:], in1=nhalf[:], op=ALU.pow).then_inc(rstd_ok, 1)

            def expand(it, g):
                pool.wait_ge(recip_ok, it.b * NG + (g + 1))
                pool.wait_ge(o_prod, it.b * NG + (g + 1))
                pool.sem_inc(carriers, 1)
                G_.tensor_copy(rexp[:], recips[:, g % 2, :].rearrange("p (c r) -> p c r", c=4).unsqueeze(3)
                               .to_broadcast([P, 4, 4, HD])).then_inc(rexp_ok, 1)

            def o_low(it, g):
                pool.wait_ge(oT_hi_ok, it.b * NG + (g + 1))
                G_.tensor_tensor(out=oT_lo[:, g, :], in0=rT[:], in1=oT_hi[:, g, :].bitcast(F32),
                                 op=ALU.subtract).then_inc(oT_done, 1)

            pool.sem_inc(oT_done, 1)
            G_.memset(ident[:], 1.0).then_inc(ready, 1)
            G_.memset(mask[:], 0.0).then_inc(ready, 1)
            G_.memset(nhalf[:], -0.5).then_inc(ready, 1)
            pool.wait_ge(ready, 3)
            G_.affine_select(out=ident[:], in_=ident[:], compare_op=ALU.is_equal, fill=0.0, base=0,
                             pattern=[[-1, P]], channel_multiplier=1).then_inc(consts, 1)
            G_.affine_select(out=mask[:, 384:512], in_=mask[:, 384:512], compare_op=ALU.is_ge, fill=MASKED, base=0,
                             pattern=[[-1, P]], channel_multiplier=1).then_inc(consts, 1)
            inverse_root(0)
            for fb in range(4):
                split_context(0, fb)

            def body(it):
                b = it.b
                expand(it, 0)
                if not it.last:
                    inverse_root(b + 1)
                o_low(it, 0)
                expand(it, 1)
                o_low(it, 1)
                if not it.last:
                    pool.wait_ge(dense, it.done("K3"))
                    split_context(b + 1, 0)
                    split_context(b + 1, 1)
                expand(it, 2)
                if not it.last:
                    split_context(b + 1, 2)
                o_low(it, 2)
                if not it.last:
                    split_context(b + 1, 3)
                pool.wait_ge(res_in, b * 16 + 16)
                for t in range(QT):
                    G_.tensor_tensor(out=xt[:, t, :], in0=xt[:, t, :], in1=bo_row[:],
                                     op=ALU.add).then_inc(res_ok, 1)
                expand(it, 3)
                o_low(it, 3)

            over_batches(pool, body)


def stage_b(nc, x1, w1, w2, vecs, b2, out):
    B, S, D = x1.shape
    F = w1.shape[1]
    KT = D // P
    FT = F // P
    QT = S // P
    WC = F // 512
    FC = FT // WC
    RING_H = 4

    with ExitStack() as ctx:
        def sb(name, shape, dt=F32):
            return ctx.enter_context(nc.sbuf_tensor(name, shape, dt))

        def pb(name):
            return ctx.enter_context(nc.psum_tensor(name, [P, 512], F32))

        def sem(name):
            return ctx.enter_context(nc.semaphore(name))

        w1_hi = sb("w1_hi", [P, KT, F], F32R)
        w1_lo = sb("w1_lo", [P, KT, F], F32R)
        w2_hi = sb("w2_hi", [P, FT, D], F32R)
        w2_lo = sb("w2_lo", [P, FT, D], F32R)
        raw = sb("raw", [P, 2, KT, 512])
        vec = sb("vecb", [P, 2 * KT + FT])
        b1s = sb("b1s", [P, FT])
        b2_row = sb("b2_row", [P, D])
        xn = sb("xn", [P, QT, D])
        xr = sb("xr", [P, QT, D])
        hT_hi = sb("hT_hi", [P, KT, S], F32R)
        hT_lo = sb("hT_lo", [P, KT, S], F32R)
        g_sb = sb("g_sb", [P, 2, S])
        g_hi = sb("g_hi", [P, RING_H, S], F32R)
        g_lo = sb("g_lo", [P, RING_H, S], F32R)
        ident = sb("identb", [P, P])
        stats = sb("statsb", [P, QT, 6])
        mv = sb("mvb", [P, QT, 2])
        ve = sb("veb", [P, QT])
        rstd = sb("rstdb", [P, QT])
        nhalf = sb("nhalfb", [P, QT])

        bank_f = [pb(f"bank_f{i}") for i in range(2)]
        bank_x = [pb(f"bank_x{i}") for i in range(2)]
        bank_o = [pb(f"bank_o{i}") for i in range(4)]

        carriers = sem("carriersb")
        vec_in, b2_in = sem("vecb_in"), sem("b2_in")
        raw_in = [sem(f"rawb_in{i}") for i in range(2)]
        xn_in, xr_in, stored = sem("xn_in"), sem("xr_in"), sem("out_stored")
        ready, consts, b1_mm, b1_ok, scaled = (sem(n) for n in ("readyb", "constsb", "b1_mm", "b1_ok", "scaledb"))
        w1_hi_ok, w1_ok, w2_hi_ok, w2_ok = (sem(n) for n in ("w1_hi_ok", "w1_ok", "w2_hi_ok", "w2_ok"))
        bn_ok, mv_ok, ve_ok, rstd_ok, xn_ok = (sem(n) for n in ("bnb_ok", "mvb_ok", "veb_ok", "rstdb_ok", "xnb_ok"))
        x_t, hT_hi_ok, hT_ok = (sem(n) for n in ("x_t", "hT_hi_ok", "hT_ok"))
        ffn1, gelu, g_hi_ok, g_ok, ffn2, summed, xr_ok = (
            sem(n) for n in ("ffn1", "gelu", "g_hi_ok", "g_ok", "ffn2", "summed", "xr_ok"))

        x_v = x1.rearrange("b (t p) d -> b p t d", p=P)
        out_v = out.rearrange("b (t p) d -> b p t d", p=P)
        w1_v = w1.rearrange("(t p) f -> p t f", p=P)
        w2_v = w2.rearrange("(c t p) d -> c p t d", p=P, t=FC)

        def over_chunks(eng, body):
            if B > 1:
                with eng.Fori(0, B - 1) as c:
                    body(c, False)
            body(B - 1, True)

        block = ctx.enter_context(nc.Block())

        @block.sync
        def _(sp):
            def one(view, b):
                return view[bass.ds(b, 1)].rearrange("o p t d -> p (o t) d")

            sp.sem_inc(stored, 16)
            sp.dma_start(xn[:], one(x_v, 0)).then_inc(xn_in, 16)
            sp.dma_start(vec[:], vecs).then_inc(vec_in, 16)
            sp.dma_start(b2_row[:], b2.partition_broadcast(P)).then_inc(b2_in, 16)
            for wc in range(WC):
                if wc > 0:
                    sp.wait_ge(w1_ok, wc)
                sp.dma_start(raw[:, 0, :, :], w1_v[:, :, 512 * wc:512 * wc + 512]).then_inc(raw_in[0], 16)
                if wc > 0:
                    sp.wait_ge(w2_ok, wc)
                sp.dma_start(raw[:, 1, :, :], w2_v[wc]).then_inc(raw_in[1], 16)

            def body(c, last):
                sp.wait_ge(stored, c * 64 + 16)
                sp.dma_start(xr[:], one(x_v, c)).then_inc(xr_in, 16)
                if not last:
                    sp.wait_ge(x_t, c * QT + QT)
                    sp.dma_start(xn[:], one(x_v, c + 1)).then_inc(xn_in, 16)
                for t in range(QT):
                    sp.wait_ge(summed, c * QT + (t + 5))
                    sp.dma_start(one(out_v, c)[:, t, :], xr[:, t, :]).then_inc(stored, 16)

            over_chunks(sp, body)
            sp.wait_ge(stored, 64 * B + 16)

        @block.tensor
        def _(pe):
            def split_product(o, lh, ll, rh, rl, first, last):
                pe.matmul(o, lh, rh, start=first, stop=False)
                pe.matmul(o, lh, rl, start=False, stop=False)
                return pe.matmul(o, ll, rh, start=False, stop=last)

            def x_transpose(m, t):
                pe.wait_ge(xn_ok, m * QT + (t + 1))
                pe.wait_ge(hT_ok, m * QT + (t + 1))
                for f in range(KT):
                    mm = pe.transpose(bank_x[t % 2][:, P * f:P * f + P], xn[:, t, P * f:P * f + P], ident[:])
                mm.then_inc(x_t, 1)

            def hidden(c, f):
                if f % FC == 0:
                    pe.wait_ge(w1_ok, f // FC + 1)
                if f == 0:
                    pe.wait_ge(hT_ok, c * QT + (QT + 2))
                pe.wait_ge(gelu, c * FT + (f + 1))
                cols = slice(P * f, P * f + P)
                for kt in range(KT):
                    mm = split_product(bank_f[f % 2][:], w1_hi[:, kt, cols], w1_lo[:, kt, cols],
                                       hT_hi[:, kt, :], hT_lo[:, kt, :], kt == 0, kt == KT - 1)
                mm.then_inc(ffn1, 1)

            def output(c, f):
                if f % FC == 0:
                    pe.wait_ge(w2_ok, f // FC + 1)
                pe.wait_ge(g_ok, c * FT + (f + 3))
                for t in range(QT):
                    if f == 0:
                        pe.wait_ge(summed, c * QT + (t + 1))
                    cols = slice(P * t, P * t + P)
                    mm = split_product(bank_o[t][:], g_hi[:, f % RING_H, cols], g_lo[:, f % RING_H, cols],
                                       w2_hi[:, f, :], w2_lo[:, f, :], f == 0, f == FT - 1)
                mm.then_inc(ffn2, 1)

            pe.sem_inc(ffn2, RING_H)
            pe.wait_ge(vec_in, 16)
            pe.wait_ge(consts, 1)
            for t in range(QT):
                x_transpose(0, t)
            for wc in range(WC):
                pe.wait_ge(raw_in[0], 16 * (wc + 1))
                for f in range(FC * wc, FC * wc + FC):
                    for kt in range(KT):
                        at = P * (f - FC * wc)
                        mm = pe.matmul(bank_o[0][:, f:f + 1], raw[:, 0, kt, at:at + P], vec[:, KT + kt:KT + kt + 1],
                                       start=(kt == 0), stop=(kt == KT - 1))
                mm.then_inc(b1_mm, 1)
            pe.wait_ge(b1_ok, WC)

            def body(c, last):
                for f in range(FT):
                    hidden(c, f)
                    if f >= 2:
                        output(c, f - 2)
                for half in range(2):
                    if not last:
                        x_transpose(c + 1, 2 * half)
                        x_transpose(c + 1, 2 * half + 1)
                    output(c, FT - 2 + half)

            over_chunks(pe, body)

        @block.vector
        def _(dve):
            V = nc.vector

            def layer_norm_stats(m):
                dve.wait_ge(xn_in, m * 16 + 16)
                for t in range(QT):
                    V.bn_stats(stats[:, t, :], xn[:, t, :]).then_inc(bn_ok, 1)
                for t in range(QT):
                    dve.wait_ge(bn_ok, m * QT + (t + 1))
                    dve.sem_inc(carriers, 1)
                    V.bn_aggr(mv[:, t, :], stats[:, t, :]).then_inc(mv_ok, 1)
                dve.wait_ge(mv_ok, m * QT + QT)
                V.tensor_scalar(ve[:], mv[:, :, 1], EPS, None, ALU.add).then_inc(ve_ok, 1)

            def normalise(m, t):
                if t == 0:
                    dve.wait_ge(rstd_ok, m + 1)
                V.tensor_scalar(xn[:, t, :], xn[:, t, :], mv[:, t, 0:1], rstd[:, t:t + 1],
                                ALU.subtract, ALU.mult).then_inc(xn_ok, 1)

            def x_low(m, t):
                dve.wait_ge(hT_hi_ok, m * QT + (t + 1))
                cols = slice(P * t, P * t + P)
                V.tensor_tensor(hT_lo[:, :, cols], bank_x[t % 2][:].rearrange("p (f c) -> p f c", f=KT),
                                hT_hi[:, :, cols].bitcast(F32), ALU.subtract).then_inc(hT_ok, 1)

            def split_gelu(c, f):
                dve.wait_ge(gelu, c * FT + (f + 3))
                dve.wait_ge(ffn2, c * FT + (f + 1))
                V.tensor_copy(g_hi[:, f % RING_H, :], g_sb[:, f % 2, :]).then_inc(g_hi_ok, 1)
                dve.wait_ge(g_hi_ok, c * FT + (f + 1))
                V.tensor_tensor(g_lo[:, f % RING_H, :], g_sb[:, f % 2, :], g_hi[:, f % RING_H, :].bitcast(F32),
                                ALU.subtract).then_inc(g_ok, 1)

            dve.sem_inc(hT_ok, 2)
            dve.sem_inc(g_ok, 2)
            dve.sem_inc(summed, QT)
            layer_norm_stats(0)
            for t in range(QT):
                normalise(0, t)
            for t in range(QT):
                x_low(0, t)
            dve.wait_ge(vec_in, 16)
            for wc in range(WC):
                dve.wait_ge(b1_mm, wc + 1)
                cols = slice(FC * wc, FC * wc + FC)
                V.tensor_tensor(b1s[:, cols], bank_o[0][:, cols], vec[:, 2 * KT + FC * wc:2 * KT + FC * wc + FC],
                                ALU.add).then_inc(b1_ok, 1)
                for kt in range(KT):
                    V.tensor_scalar(raw[:, 0, kt, :], raw[:, 0, kt, :], vec[:, kt:kt + 1], None,
                                    ALU.mult).then_inc(scaled, 1)
                dve.wait_ge(w1_hi_ok, wc + 1)
                fs = slice(512 * wc, 512 * wc + 512)
                V.tensor_tensor(w1_lo[:, :, fs], raw[:, 0, :, :], w1_hi[:, :, fs].bitcast(F32),
                                ALU.subtract).then_inc(w1_ok, 1)
                dve.wait_ge(w2_hi_ok, wc + 1)
                V.tensor_tensor(w2_lo[:, cols, :], raw[:, 1, :, :], w2_hi[:, cols, :].bitcast(F32),
                                ALU.subtract).then_inc(w2_ok, 1)

            def body(c, last):
                for f in range(FT):
                    split_gelu(c, f)
                    if not last:
                        if f == 2:
                            layer_norm_stats(c + 1)
                        if f in (5, 6, 7, 8):
                            normalise(c + 1, f - 5)
                if not last:
                    for t in range(QT):
                        x_low(c + 1, t)
                dve.wait_ge(ffn2, c * FT + (FT + RING_H))
                for t in range(QT):
                    dve.wait_ge(xr_ok, c * QT + (t + 1))
                    V.tensor_tensor(xr[:, t, :], bank_o[t][:], xr[:, t, :], ALU.add).then_inc(summed, 1)

            over_chunks(dve, body)

        @block.scalar
        def _(act):
            A = nc.scalar

            def x_high(m, t):
                act.wait_ge(x_t, m * QT + (t + 1))
                A.copy(hT_hi[:, :, P * t:P * t + P],
                       bank_x[t % 2][:].rearrange("p (f c) -> p f c", f=KT)).then_inc(hT_hi_ok, 1)

            act.sem_inc(gelu, 2)
            for t in range(QT):
                x_high(0, t)
            for wc in range(WC):
                fs = slice(512 * wc, 512 * wc + 512)
                act.wait_ge(scaled, KT * (wc + 1))
                A.copy(w1_hi[:, :, fs], raw[:, 0, :, :]).then_inc(w1_hi_ok, 1)
                act.wait_ge(raw_in[1], 16 * (wc + 1))
                A.copy(w2_hi[:, FC * wc:FC * wc + FC, :], raw[:, 1, :, :]).then_inc(w2_hi_ok, 1)

            def body(c, last):
                for f in range(FT):
                    act.wait_ge(ffn1, c * FT + (f + 1))
                    act.wait_ge(g_ok, c * FT + (f + 1))
                    A.activation(g_sb[:, f % 2, :], bank_f[f % 2][:], ACT.Gelu, bias=b1s[:, f:f + 1],
                                 scale=1.0).then_inc(gelu, 1)
                if not last:
                    for t in range(QT):
                        x_high(c + 1, t)

            over_chunks(act, body)

        @block.gpsimd
        def _(pool):
            G_ = nc.gpsimd

            def inverse_root(m):
                pool.wait_ge(ve_ok, m + 1)
                G_.tensor_tensor(out=rstd[:], in0=ve[:], in1=nhalf[:], op=ALU.pow).then_inc(rstd_ok, 1)

            G_.memset(ident[:], 1.0).then_inc(ready, 1)
            G_.memset(nhalf[:], -0.5).then_inc(ready, 1)
            pool.wait_ge(ready, 2)
            G_.affine_select(out=ident[:], in_=ident[:], compare_op=ALU.is_equal, fill=0.0, base=0,
                             pattern=[[-1, P]], channel_multiplier=1).then_inc(consts, 1)
            inverse_root(0)
            pool.wait_ge(b2_in, 16)

            def body(c, last):
                pool.wait_ge(xr_in, c * 16 + 16)
                for t in range(QT):
                    G_.tensor_tensor(out=xr[:, t, :], in0=xr[:, t, :], in1=b2_row[:], op=ALU.add).then_inc(xr_ok, 1)
                if not last:
                    inverse_root(c + 1)

            over_chunks(pool, body)


def build(nc, x, ctxT, wq, wk, wv, wo, vecs_a, bo, w1, w2, vecs_b, b2, out):
    x1 = nc.dram_tensor("x1_scratch", tuple(x.shape), F32).ap()
    stage_a(nc, x, ctxT, wq, wk, wv, wo, vecs_a, bo, x1)
    stage_b(nc, x1, w1, w2, vecs_b, b2, out)


def kernel(x, ctx_1024, **w):
    import numpy as np
    import concourse.bacc as bacc
    from concourse.bass_utils import run_bass_kernel_spmd

    w = {k.replace("L0_xattn_", ""): np.asarray(v) for k, v in w.items()}
    D = x.shape[-1]

    def by_columns(v):
        return np.asarray(v).reshape(-1, P).T

    def feature_major(v):
        return v.reshape(*v.shape[:-1], HEADS // 4, 4, D // HEADS).swapaxes(-1, -2).reshape(v.shape)

    arrays = {
        "x": np.asarray(x),
        "ctxT": np.asarray(ctx_1024).transpose(0, 2, 1),
        "wq": feature_major(w["wq"]),
        "wk": feature_major(w["wk"]),
        "wv": w["wv"],
        "wo": w["wo"],
        "vecs_a": np.stack([by_columns(v) for v in (w["ln1_g"], w["ln1_b"], feature_major(w["bq"]),
                                                    feature_major(w["bk"]), w["bv"])], axis=1),
        "bo": w["bo"],
        "w1": w["w1"],
        "w2": w["w2"],
        "vecs_b": np.concatenate([by_columns(w["ln2_g"]), by_columns(w["ln2_b"]), by_columns(w["b1"])], axis=1),
        "b2": w["b2"],
    }
    nc = bacc.Bacc("TRN2", target_bir_lowering=False, num_devices=1)
    arrays = {f"in_{k}": np.ascontiguousarray(v) for k, v in arrays.items()}
    args = [nc.dram_tensor(k, v.shape, mybir.dt.from_np(v.dtype), kind="ExternalInput").ap()
            for k, v in arrays.items()]
    out = nc.dram_tensor("out", x.shape, F32, kind="ExternalOutput").ap()
    build(nc, *args, out)
    r = run_bass_kernel_spmd(nc, [arrays], core_ids=[0])
    return r.results[0]["out"]
```

```python
from contextlib import ExitStack

import concourse.bass as bass
from concourse import mybir
from concourse.alu_op_type import AluOpType as ALU

ACT = mybir.ActivationFunctionType
F32 = mybir.dt.float32
F32R = mybir.dt.float32r
BF16 = mybir.dt.bfloat16

P = 128
EPS = 1e-5
MASKED = 3.0e38

HEADS = 16
BANKS_S = 3
SLOTS_S = 4
LAG = 3
POS = [0, 1, 3, 2]


def tile_of(k):
    if k < 4:
        return 0, k, (0, 1)
    return 1, (k - 4) // 2, (2 + (k - 4) % 2,)


def act_moves(k):
    return k >= 4 and (k - 4) % 2 == 1


def stage_a(nc, x, ctxT, wq, wk, wv, wo, vecs, bo, x1):
    B, S, D = x.shape
    HD = D // HEADS
    KT = D // P
    QT = S // P
    NG = HEADS // 4
    TG = 12
    TB = NG * TG
    SCALE = float(HD) ** -0.5

    PRO = ["X0", "X1", "X2", "X3", "Q0", "K0", "V0a", "V1a", "V3a"]

    R_AT = 5

    def plan(first, last):
        steps = [[] for _ in range(TB)]

        def add(job, g, ks, each=12):
            for i, k in enumerate(ks):
                steps[TG * g + k].append((job, i * each, i * each + each))

        for g in range(NG):
            if g < NG - 1 or not last:
                add(f"Q{(g + 1) % NG}", g, (0, 1, 2), 4)
                add(f"K{(g + 1) % NG}", g, (2, 3, 4), 4)
            if g > 0 or not first:
                add("R", g, (R_AT,))
        add("V2a", 0, (6, 7), 6)
        if not first:
            add("O0", 0, (10, 11), 6)
            add("O1", 1, (5, 6), 6)
            add("O2", 1, (7, 8), 6)
            add("O3", 1, (8, 9), 6)
        add("V0b", 1, (10,))
        add("V1b", 1, (11,))
        add("V2b", 2, (6,))
        add("V3b", 2, (7,))
        if not last:
            for t in range(QT):
                add(f"X{t}", 2, (8 + t,))
            add("V0a", 3, (6, 7), 6)
            add("V1a", 3, (8, 9), 6)
            add("V3a", 3, (10, 11), 6)
        return steps

    TAIL = [[], [], [], [], [], [("R", 0, 12)], [], [], [("O0", 0, 12)], [("O1", 0, 12)], [("O2", 0, 12)],
            [("O3", 0, 12)]]
    assert B > 2

    with ExitStack() as ctx:
        def sb(name, shape, dt=F32):
            return ctx.enter_context(nc.sbuf_tensor(name, shape, dt))

        def pb(name):
            return ctx.enter_context(nc.psum_tensor(name, [P, 512], F32))

        def sem(name):
            return ctx.enter_context(nc.semaphore(name))

        w_hi = [sb(f"{n}_hi", [P, KT, D], F32R) for n in ("wq", "wk", "wv", "wo")]
        w_lo = [sb(f"{n}_lo", [P, KT, D], F32R) for n in ("wq", "wk", "wv", "wo")]
        vec = sb("vec", [P, 5, 4])
        bqs = sb("bqs", [P, NG])
        bo_row = sb("bo_row", [P, D])
        xt = sb("xt", [P, QT, D])
        xnT_hi = sb("xnT_hi", [P, KT, S], F32R)
        xnT_lo = sb("xnT_lo", [P, KT, S], F32R)
        c_raw = sb("c_raw", [P, 2, S])
        cT_hi = sb("cT_hi", [P, KT, S], F32R)
        cT_lo = sb("cT_lo", [P, KT, S], F32R)
        st_hi = sb("st_hi", [P, 2, S], F32R)
        st_lo = sb("st_lo", [P, 2, S], F32R)
        stack = sb("stack", [P, 2, 2, 4, S], F32R)
        v_sb = sb("v_sb", [P, QT, D])
        sm = sb("sm", [P, SLOTS_S, 512])
        pT = sb("pT", [P, 4, 1280])
        rT = sb("rT", [P, 512])
        oT_hi = sb("oT_hi", [P, NG, S], F32R)
        oT_lo = sb("oT_lo", [P, NG, S], F32R)
        mask = sb("mask", [P, 512], BF16)
        ident = sb("ident", [P, P])
        mins = sb("mins", [P, 2, 16])
        sums = sb("sums", [P, 2, 16])
        recips = sb("recips", [P, 2, 16])
        stats = sb("stats", [P, QT, 6])
        mv = sb("mv", [P, QT, 2])
        ve = sb("ve", [P, QT])
        rstd = sb("rstd", [P, QT])
        nhalf = sb("nhalf", [P, QT])
        raw = pT[:].rearrange("p a b -> p (a b)")
        bvx = sm[:, 0, :].rearrange("p (t m) -> p t m", t=KT)

        bank_s = [pb(f"bank_s{i}") for i in range(BANKS_S)]
        bank_t = [pb(f"bank_t{i}") for i in range(2)]
        bank_v = pb("bank_v")
        bank_d = [pb(f"bank_d{i}") for i in range(2)]

        vec_in, bo_in = sem("vec_in"), sem("bo_in")
        raw_in = [sem(f"raw_in{i}") for i in range(4)]
        x_in, res_in, stored = sem("x_in"), sem("res_in"), sem("stored")
        c_in = [sem(f"c_in{i}") for i in range(2)]
        stacked = sem("stacked")
        carriers = sem("carriers")
        ready = sem("ready")
        consts, bias_mm, scaled, w_hi_done, w_lo_done, bvx_ok, bias_ok = (
            sem(n) for n in ("consts", "bias_mm", "scaled", "w_hi_done", "w_lo_done", "bvx_ok", "bias_ok"))
        scored, masked, probs, transposed, pv_done = (
            sem(n) for n in ("scored", "masked", "probs", "transposed", "pv_done"))
        moved = [sem(f"moved{i}") for i in range(2)]
        recip_ok, rexp_ok, o_prod, oT_hi_ok, oT_done = (
            sem(n) for n in ("recip_ok", "rexp_ok", "o_prod", "oT_hi_ok", "oT_done"))
        dense = sem("dense")
        d_free = [sem(f"d_free{i}") for i in range(2)]
        qk_hi, x_hi = sem("qk_hi"), sem("x_hi")
        bn_ok, mv_ok, ve_ok, rstd_ok, xn_ok, c_hi_ok, c_done, res_ok = (
            sem(n) for n in ("bn_ok", "mv_ok", "ve_ok", "rstd_ok", "xn_ok", "c_hi_ok", "c_done", "res_ok"))

        def jobs_of(steps):
            order, ends = [], {}
            for n, slot in enumerate(steps):
                for job, first, _ in slot:
                    if first == 0:
                        order.append((job, n // TG))
                    ends[job, n // TG] = n
            return order, ends

        class Iteration:
            def __init__(self, b, start, steps, per_batch=0, first=False, last=False, tail=False):
                self.b, self.start, self.steps, self.per_batch = b, start, steps, per_batch
                self.first, self.last, self.tail = first, last, tail
                self.order, self.ends = jobs_of(steps)
            def place(self, job, g):
                if g < 0:
                    return {"V0a": -3, "V1a": -2, "V3a": -1}[job]
                return self.order.index((job, g))
            def bank(self, job, g):
                return (self.start + self.place(job, g)) % 2
            def done(self, job, g):
                return self.b * self.per_batch + (self.start + self.place(job, g) + 1)
            def bank_wait(self, job, g):
                return self.b * (self.per_batch // 2) + ((self.start + self.place(job, g)) // 2 + 1)
            def bank_read(self, job, g):
                return self.b * (self.per_batch // 2) + ((self.start + self.place(job, g)) // 2 + 2)
            def ended(self, n):
                return [job for job, at in self.ends.items() if at == n]

        def count(steps):
            return len(jobs_of(steps)[0])

        pro = Iteration(0, 0, [[(job, 0, 12)] for job in PRO], first=True)
        first_plan, mid_plan, last_plan = plan(True, False), plan(False, False), plan(False, True)
        PER = count(mid_plan)
        assert PER % 2 == 0
        mid_start = len(PRO) + count(first_plan)

        def over_batches(eng, body):
            body(Iteration(0, len(PRO), first_plan, first=True))
            with eng.Fori(1, B - 1) as b:
                body(Iteration(b, mid_start - PER, mid_plan, per_batch=PER))
            last_start = mid_start + (B - 2) * PER
            body(Iteration(B - 1, last_start, last_plan, last=True))
            body(Iteration(B, last_start + count(last_plan), TAIL, tail=True))

        x_v = x.rearrange("b (t p) d -> b p t d", p=P)
        x1_v = x1.rearrange("b (t p) d -> b p t d", p=P)
        c_v = ctxT.rearrange("b (t p) s -> b p t s", p=P)

        block = ctx.enter_context(nc.Block())

        @block.sync
        def _(sp):
            def one(view, b):
                return view[bass.ds(b, 1)].rearrange("o p t d -> p (o t) d")

            def load_c(m, fb):
                sp.dma_start(c_raw[:, fb % 2, :], one(c_v, m)[:, fb, :]).then_inc(c_in[fb % 2], 16)

            def stack_parts(it, w, job, g, par):
                sp.wait_ge(d_free[it.bank(job, g)], it.bank_read(job, g))
                for part, src in enumerate(((st_hi, st_hi, st_lo, st_lo), (st_hi, st_lo, st_hi, st_lo))[w]):
                    sp.dma_start(stack[32 * part:32 * part + 32, par, w, :, :].bitcast(F32),
                                 src[:, w, :].bitcast(F32)).then_inc(stacked, 16)

            sp.sem_inc(stored, 16)
            sp.dma_start(vec[:], vecs).then_inc(vec_in, 16)
            sp.dma_start(xt[:], one(x_v, 0)).then_inc(x_in, 16)
            sp.dma_start(bo_row[:], bo.partition_broadcast(P)).then_inc(bo_in, 16)
            for i, w in enumerate((wq, wk)):
                sp.dma_start(raw[:, 2048 * i:2048 * i + 2048].rearrange("p (t n) -> p t n", t=KT),
                             w.rearrange("(t p) n -> p t n", p=P)).then_inc(raw_in[i], 16)
            load_c(0, 0)
            load_c(0, 1)
            for i, w in enumerate((wv, wo)):
                sp.wait_ge(w_lo_done, i + 1)
                sp.dma_start(raw[:, 2048 * i:2048 * i + 2048].rearrange("p (t n) -> p t n", t=KT),
                             w.rearrange("(t p) n -> p t n", p=P)).then_inc(raw_in[i + 2], 16)
                sp.wait_ge(c_done, i + 1)
                load_c(0, 2 + i)
            for w, job in enumerate(("Q0", "K0")):
                stack_parts(pro, w, job, 0, 0)

            def stacks(it, g):
                if g > 0:
                    sp.wait_ge(scored, it.b * TB + TG * g)
                    sp.sem_inc(carriers, 1)
                elif not it.first:
                    sp.wait_ge(scored, it.b * TB)
                    sp.sem_inc(carriers, 1)
                for w, name in enumerate("QK"):
                    stack_parts(it, w, f"{name}{(g + 1) % NG}", g, (g + 1) % 2)

            def store(it, t):
                g = 0 if it.tail or t == 0 else 1
                sp.wait_ge(d_free[it.bank(f"O{t}", g)], it.bank_read(f"O{t}", g))
                sp.dma_start(one(x1_v, it.b - 1)[:, t, :], xt[:, t, :]).then_inc(stored, 16)

            def body(it):
                b = it.b
                if it.tail:
                    for t in range(QT):
                        store(it, t)
                    return
                if not it.last:
                    sp.wait_ge(c_done, b * 4 + 4)
                    load_c(b + 1, 0)
                    load_c(b + 1, 1)
                for g in range(2):
                    stacks(it, g)
                    if not it.first:
                        for t in ((0,), (1, 2, 3))[g]:
                            store(it, t)
                if it.first:
                    sp.wait_ge(dense, pro.done("X3", 0))
                else:
                    sp.wait_ge(stored, b * 64 + 16)
                if not it.last:
                    sp.dma_start(xt[:], one(x_v, b + 1)).then_inc(x_in, 16)
                stacks(it, 2)
                if not it.last:
                    sp.wait_ge(c_done, b * 4 + 5)
                    load_c(b + 1, 2)
                    sp.wait_ge(dense, it.done("X3", 2))
                sp.dma_start(xt[:], one(x_v, b)).then_inc(res_in, 16)
                if not it.last:
                    sp.wait_ge(c_done, b * 4 + 6)
                    load_c(b + 1, 3)
                    stacks(it, 3)

            over_batches(sp, body)
            sp.wait_ge(stored, 64 * B + 16)

        @block.tensor
        def _(pe):
            def split_product(out, lh, ll, rh, rl, first, last):
                pe.matmul(out, lh, rh, start=first, stop=False)
                pe.matmul(out, lh, rl, start=False, stop=False)
                return pe.matmul(out, ll, rh, start=False, stop=last)

            def dense_step(it, job, g, i, j):
                kind, bank = job[0], bank_d[it.bank(job, g)]
                if i == 0:
                    pe.wait_ge(d_free[it.bank(job, g)], it.bank_wait(job, g))
                if kind == "X":
                    t, m = int(job[1]), (0 if it is pro else it.b + 1)
                    pe.wait_ge(xn_ok, m * QT + (t + 1))
                    for f in range(KT):
                        mm = pe.transpose(bank[:, P * f:P * f + P], xt[:, t, P * f:P * f + P], ident[:])
                elif kind == "R":
                    pe.wait_ge(rexp_ok, it.b * NG + g)
                    for c in range(QT):
                        mm = pe.transpose(bank[:, P * c:P * c + P],
                                          rT[:, P * c:P * c + P], ident[:])
                else:
                    t = int(job[1])
                    if i == 0 and job == "O0":
                        pe.wait_ge(oT_done, it.b * NG + 1)
                    if i == 0 and job == "Q0":
                        for x in ("X2", "X3"):
                            xg = 0 if it is pro else 2
                            pe.wait_ge(d_free[it.bank(x, xg)], it.bank_read(x, xg))
                    for n in range(i, j):
                        kt, part = divmod(n, 3)
                        if job == "K0" and part == 0:
                            pe.wait_ge(c_done, (0 if it is pro else it.b * 4 + 4) + (kt + 1))
                        tokens = slice(P * t, P * t + P)
                        if kind == "Q":
                            left, right, lc, rc = w_of[0], xnT, tokens, slice(0, S)
                        elif kind == "K":
                            left, right, lc, rc = w_of[1], cT, tokens, slice(0, S)
                        elif kind == "V":
                            half = 256 * "ab".index(job[2])
                            left, right, lc, rc = cT, w_of[2], tokens, slice(half, half + 256)
                        else:
                            left, right, lc, rc = oT, w_of[3], slice(P * POS[t], P * POS[t] + P), slice(0, D)
                        mm = pe.matmul(bank[:, 0:rc.stop - rc.start], left[part // 2][:, kt, lc],
                                       right[part % 2][:, kt, rc], start=(n == 0), stop=(n == 11))
                if j == 12:
                    mm.then_inc(dense, 1)

            def score(it, n):
                g, k = divmod(n, TG)
                _, r, qts = tile_of(k)
                if k == 0:
                    pe.wait_ge(stacked, it.b * (128 * NG) + 128 * (g + 1))
                pe.wait_ge(masked, it.b * TB + (n + 1))
                off = 0
                for qt in qts:
                    w = P * (qt + 1)
                    mm = pe.matmul(bank_s[n % BANKS_S][:, off:off + w], stack[:, g % 2, 0, r, P * qt:P * qt + P],
                                   stack[:, g % 2, 1, r, 0:w], start=True, stop=True)
                    off += w
                mm.then_inc(scored, 1)

            def p_transpose(it, n):
                k = n % TG
                _, r, qts = tile_of(k)
                pe.wait_ge(probs, it.b * TB + (n + 1))
                pe.wait_ge(moved[n % 2], it.b * (TB // 2) + (n // 2 + 1))
                for c in range(sum(qt + 1 for qt in qts)):
                    mm = pe.transpose(bank_t[n % 2][:, P * c:P * c + P], sm[:, n % SLOTS_S, P * c:P * c + P], ident[:])
                mm.then_inc(transposed, 1)

            def pv(it, g, pair):
                last_tile = TG * g + (3 if pair == 0 else 11)
                for i in range(2):
                    pe.wait_ge(moved[i], it.b * (TB // 2) + ((last_tile + 1) // 2 + 1))
                if pair == 0:
                    pe.wait_ge(o_prod, it.b * NG + (g + 1))
                if g in (0, 2):
                    for t in (2 * pair, 2 * pair + 1):
                        name = f"V{t}{'ab'[g // 2]}"
                        beside = {"V2a": 0, "V0b": 1, "V1b": 1, "V2b": 2, "V3b": 2}.get(name, -1)
                        pe.wait_ge(d_free[it.bank(name, beside)], it.bank_read(name, beside))
                if pair == 0:
                    parts = [(0, 0, 256, 0), (1, 256, 128, 128)]
                else:
                    parts = [(0, 384, 256, 256), (1, 640, 256, 256), (2, 896, 256, 256), (3, 1152, 128, 256)]
                for j, at, w, to in parts:
                    for r in range(4):
                        h = 4 * (g % NG) + r
                        mm = pe.matmul(bank_v[32 * r:32 * r + 32, to:to + w], v_sb[:, j, HD * h:HD * h + HD],
                                       pT[:, r, at:at + w], start=(j == 0), stop=(j == len(parts) - 1),
                                       skip_group_check=True)
                mm.then_inc(pv_done, 1)

            w_of = list(zip(w_hi, w_lo))
            xnT, cT, oT = (xnT_hi, xnT_lo), (cT_hi, cT_lo), (oT_hi, oT_lo)

            pe.sem_inc(transposed, SLOTS_S)
            pe.sem_inc(pv_done, 2)
            pe.wait_ge(vec_in, 16)
            pe.wait_ge(raw_in[0], 16)
            for g in range(NG):
                for kt in range(KT):
                    mm = pe.matmul(bank_s[0][:, g:g + 1], raw[:, D * kt + P * g:D * kt + P * g + P],
                                   vec[:, 1, kt:kt + 1], start=(kt == 0), stop=(kt == KT - 1))
            mm.then_inc(bias_mm, 1)
            pe.wait_ge(consts, 1)
            for job in PRO:
                if job == "Q0":
                    pe.wait_ge(w_lo_done, 1)
                if job == "K0":
                    pe.wait_ge(w_lo_done, 2)
                if job == "V0a":
                    pe.wait_ge(w_lo_done, 3)
                dense_step(pro, job, 0, 0, 12)
            pe.wait_ge(bvx_ok, 1)
            pe.wait_ge(raw_in[3], 16)
            for kt in range(KT):
                mm = pe.matmul(bank_s[1][:], bvx[:, kt, :], raw[:, 2048 + D * kt:2048 + D * kt + D],
                               start=(kt == 0), stop=(kt == KT - 1))
            mm.then_inc(bias_mm, 1)
            pe.wait_ge(w_lo_done, 4)
            pe.wait_ge(bias_ok, 2)

            def body(it):
                for n, steps in enumerate(it.steps):
                    g, k = divmod(n, TG)
                    if not it.tail:
                        score(it, n)
                    for job, i, j in steps:
                        dense_step(it, job, g, i, j)
                    if k == LAG + 2 and not (it.first and g == 0):
                        pv(it, g - 1, 1)
                    if k == LAG + 5 and not it.tail:
                        pv(it, g, 0)
                    if n >= LAG and not it.tail or n < LAG and not it.first:
                        p_transpose(it, n - LAG)

            over_batches(pe, body)

        def move_tile(eng, copy, it, n):
            g, k = divmod(n, TG)
            pair, r, qts = tile_of(k)
            eng.wait_ge(transposed, it.b * TB + (n + 1 + SLOTS_S))
            eng.wait_ge(pv_done, it.b * (2 * NG) + (2 * g + pair + 1))
            bank = bank_t[n % 2]
            if pair == 0:
                out, src = pT[:, r, 0:384], bank[:, 0:384]
            else:
                qt = qts[0]
                first = 0 if qt == 3 else P
                out = pT[:, r, 384:1280].rearrange("p (c q) -> p c q", q=P)[:, first // P::2, :]
                src = bank[:, 0:P * (qt + 1)].rearrange("p (c q) -> p c q", q=P)
            copy(out, src).then_inc(moved[n % 2], 1)

        @block.vector
        def _(dve):
            V = nc.vector

            def layer_norm_stats(m, t):
                if t == 0:
                    dve.wait_ge(x_in, m * 16 + 16)
                V.bn_stats(stats[:, t, :], xt[:, t, :]).then_inc(bn_ok, 1)
                if t < QT - 1:
                    return
                for t in range(QT):
                    dve.wait_ge(bn_ok, m * QT + (t + 1))
                    dve.sem_inc(carriers, 1)
                    V.bn_aggr(mv[:, t, :], stats[:, t, :]).then_inc(mv_ok, 1)
                dve.wait_ge(mv_ok, m * QT + QT)
                V.tensor_scalar(ve[:], mv[:, :, 1], EPS, None, ALU.add).then_inc(ve_ok, 1)

            def normalise(m, t):
                if t == 0:
                    dve.wait_ge(rstd_ok, m + 1)
                V.tensor_scalar(xt[:, t, :], xt[:, t, :], mv[:, t, 0:1], rstd[:, t:t + 1],
                                ALU.subtract, ALU.mult).then_inc(xn_ok, 1)

            def x_low(it, job, g, m):
                t = int(job[1])
                dve.wait_ge(x_hi, m * QT + (t + 1))
                cols = slice(P * t, P * t + P)
                V.tensor_tensor(xnT_lo[:, :, cols], bank_d[it.bank(job, g)][:].rearrange("p (f c) -> p f c", f=KT),
                                xnT_hi[:, :, cols].bitcast(F32), ALU.subtract).then_inc(d_free[it.bank(job, g)], 1)

            def qk_low(it, job, g, G):
                w, hg, bank = "QK".index(job[0]), int(job[1]), it.bank(job, g)
                dve.wait_ge(qk_hi, G * 2 + (w + 1))
                bias = bqs[:, hg:hg + 1] if w == 0 else vec[:, 3, hg:hg + 1]
                V.scalar_tensor_tensor(st_lo[:, w, :], bank_d[bank][:], bias, st_hi[:, w, :].bitcast(F32),
                                       ALU.add, ALU.subtract).then_inc(d_free[bank], 1)

            def mask_and_max(it, n):
                g, k = divmod(n, TG)
                _, r, qts = tile_of(k)
                dve.wait_ge(scored, it.b * TB + (n + 1))
                dve.wait_ge(transposed, it.b * TB + (n + 1))
                dve.sem_inc(carriers, 1)
                off = 0
                for qt in qts:
                    w = P * (qt + 1)
                    c = 4 * POS[qt] + r
                    op = V.tensor_tensor_reduce(sm[:, n % SLOTS_S, off:off + w], bank_s[n % BANKS_S][:, off:off + w],
                                                mask[:, 512 - w:512], 1.0, 0.0, ALU.add, ALU.min,
                                                mins[:, g % 2, c:c + 1])
                    off += w
                op.then_inc(masked, 1)

            def o_product(it, g):
                dve.wait_ge(d_free[it.bank("R", g + 1)], it.bank_read("R", g + 1))
                dve.wait_ge(pv_done, it.b * (2 * NG) + (2 * g + 4))
                V.tensor_tensor(rT[:], bank_v[:], rT[:], ALU.mult).then_inc(o_prod, 1)

            dve.sem_inc(masked, 3)
            dve.sem_inc(o_prod, 1)
            for i in range(2):
                dve.sem_inc(moved[i], 1)
                dve.sem_inc(d_free[i], 1)
            dve.wait_ge(vec_in, 16)
            V.tensor_copy(bvx, vec[:, 4, :].unsqueeze(2).to_broadcast([P, KT, P])).then_inc(bvx_ok, 1)
            for t in range(QT):
                layer_norm_stats(0, t)
            dve.wait_ge(bias_mm, 1)
            V.tensor_tensor(bqs[:], bank_s[0][:, 0:NG], vec[:, 2, :], ALU.add).then_inc(bias_ok, 1)
            for t in range(QT):
                normalise(0, t)
            dve.wait_ge(raw_in[0], 16)
            for kt in range(KT):
                V.tensor_scalar(raw[:, D * kt:D * kt + D], raw[:, D * kt:D * kt + D], vec[:, 0, kt:kt + 1], -SCALE,
                                ALU.mult, ALU.mult).then_inc(scaled, 1)
            dve.wait_ge(bias_ok, 1)
            V.tensor_scalar(bqs[:], bqs[:], -SCALE, None, ALU.mult).then_inc(scaled, 1)
            for i in range(4):
                dve.wait_ge(w_hi_done, i + 1)
                at = 2048 * (i % 2)
                V.tensor_tensor(w_lo[i][:].rearrange("p t n -> p (t n)"), raw[:, at:at + 2048],
                                w_hi[i][:].rearrange("p t n -> p (t n)").bitcast(F32),
                                ALU.subtract).then_inc(w_lo_done, 1)
                if i == 0:
                    for t in range(QT):
                        x_low(pro, f"X{t}", 0, 0)
                    dve.wait_ge(scaled, KT + 1)
                    qk_low(pro, "Q0", 0, 0)
            qk_low(pro, "K0", 0, 0)
            dve.wait_ge(bias_mm, 2)
            dve.wait_ge(bo_in, 16)
            V.tensor_tensor(bo_row[:], bank_s[1][:], bo_row[:], ALU.add).then_inc(bias_ok, 1)
            dve.wait_ge(consts, 2)

            def body(it):
                for n in range(len(it.steps) + it.tail):
                    g, k = divmod(n, TG)
                    if not it.tail:
                        mask_and_max(it, n)
                    if (n > LAG and not it.tail or n <= LAG and not it.first) and not act_moves((n - LAG - 1) % TG):
                        move_tile(dve, V.tensor_copy, it, n - LAG - 1)
                    beside_previous = g < NG and not (it.first and g == 0) and n < len(it.steps)
                    if k == 1 and beside_previous:
                        dve.wait_ge(probs, it.b * TB + TG * g)
                        V.reciprocal(recips[:, (g - 1) % 2, :], sums[:, (g - 1) % 2, :]).then_inc(recip_ok, 1)
                    if k == R_AT + 1 and beside_previous:
                        o_product(it, g - 1)
                    if not it.last and not it.tail and g == 2:
                        if k in (2, 3, 4, 5):
                            layer_norm_stats(it.b + 1, k - 2)
                        if k in (7, 8):
                            normalise(it.b + 1, 2 * k - 14)
                            normalise(it.b + 1, 2 * k - 13)
                    for job, jg in it.ended(n - 1):
                        if job[0] == "X":
                            x_low(it, job, jg, it.b + 1)
                        if job[0] in "QK":
                            qk_low(it, job, jg, it.b * NG + (jg + 1))
                    for job, jg in it.ended(n):
                        if job[0] == "O":
                            t, bank = int(job[1]), it.bank(job, jg)
                            dve.wait_ge(dense, it.done(job, jg))
                            dve.wait_ge(res_ok, it.b * QT + (t + 1 - QT))
                            V.tensor_tensor(xt[:, t, :], bank_d[bank][:], xt[:, t, :],
                                            ALU.add).then_inc(d_free[bank], 1)

            over_batches(dve, body)

        @block.scalar
        def _(act):
            A = nc.scalar

            def x_high(it, job, g):
                t = int(job[1])
                act.wait_ge(dense, it.done(job, g))
                A.copy(xnT_hi[:, :, P * t:P * t + P],
                       bank_d[it.bank(job, g)][:].rearrange("p (f c) -> p f c", f=KT)).then_inc(x_hi, 1)

            def qk_high(it, job, g, G):
                w, hg, bank = "QK".index(job[0]), int(job[1]), it.bank(job, g)
                act.wait_ge(dense, it.done(job, g))
                if it is not pro:
                    act.wait_ge(stacked, G * 128)
                bias = bqs[:, hg:hg + 1] if w == 0 else vec[:, 3, hg:hg + 1]
                A.activation(st_hi[:, w, :], bank_d[bank][:], ACT.Identity, bias=bias,
                             scale=1.0).then_inc(qk_hi, 1)

            def v_copy(it, job, g):
                t, half, bank = int(job[1]), "ab".index(job[2]), it.bank(job, g)
                act.wait_ge(dense, it.done(job, g))
                ahead = 1 if g == NG - 1 else 0
                if not (it.first and not ahead):
                    act.wait_ge(pv_done, it.b * (2 * NG) + (2 * NG * (ahead - 1) + 4 * half + 6))
                A.copy(v_sb[:, t, 256 * half:256 * half + 256], bank_d[bank][:, 0:256]).then_inc(d_free[bank], 1)

            def exponential(it, n):
                g, k = divmod(n, TG)
                _, r, qts = tile_of(k)
                act.wait_ge(masked, it.b * TB + (n + 4))
                off = 0
                for qt in qts:
                    w = P * (qt + 1)
                    c = 4 * POS[qt] + r
                    row = sm[:, n % SLOTS_S, off:off + w]
                    op = A.activation(row, row, ACT.Exp, bias=mins[:, g % 2, c:c + 1], scale=-1.0,
                                      accum_out=sums[:, g % 2, c:c + 1])
                    off += w
                op.then_inc(probs, 1)

            def r_copy(it, g):
                bank = it.bank("R", g + 1)
                act.wait_ge(dense, it.done("R", g + 1))
                A.copy(rT[:], bank_d[bank][:]).then_inc(d_free[bank], 1)

            def o_high(it, g):
                act.wait_ge(o_prod, it.b * NG + (g + 2))
                if g == 0 and not it.first:
                    act.wait_ge(dense, it.done("O3", 1))
                A.copy(oT_hi[:, g % NG, :], rT[:]).then_inc(oT_hi_ok, 1)

            for i in range(4):
                act.wait_ge(raw_in[i], 16)
                if i == 0:
                    act.wait_ge(scaled, KT)
                at = 2048 * (i % 2)
                A.copy(w_hi[i][:].rearrange("p t n -> p (t n)"), raw[:, at:at + 2048]).then_inc(w_hi_done, 1)
                if i == 0:
                    for t in range(QT):
                        x_high(pro, f"X{t}", 0)
                    act.wait_ge(scaled, KT + 1)
                    qk_high(pro, "Q0", 0, 0)
            qk_high(pro, "K0", 0, 0)
            v_copy(pro, "V0a", 0)
            v_copy(pro, "V1a", 0)
            v_copy(pro, "V3a", 0)

            def body(it):
                for n in range(len(it.steps)):
                    g, k = divmod(n, TG)
                    if not it.tail:
                        exponential(it, n)
                    if (n > LAG and not it.tail or n <= LAG and not it.first) and act_moves((n - LAG - 1) % TG):
                        move_tile(act, A.copy, it, n - LAG - 1)
                    if not (it.first and g == 0):
                        if k == R_AT:
                            r_copy(it, g - 1)
                        if k == (10 if g == 1 else R_AT + 2):
                            o_high(it, g - 1)
                    for job, jg in it.ended(n):
                        if job[0] == "X":
                            x_high(it, job, jg)
                        if job[0] in "QK":
                            qk_high(it, job, jg, it.b * NG + (jg + 1))
                        if job[0] == "V":
                            v_copy(it, job, jg)

            over_batches(act, body)

        @block.gpsimd
        def _(pool):
            G_ = nc.gpsimd

            def split_context(m, fb):
                pool.wait_ge(c_in[fb % 2], m * 32 + 16 * (fb // 2 + 1))
                pool.sem_inc(carriers, 1)
                G_.tensor_copy(cT_hi[:, fb, :], c_raw[:, fb % 2, :]).then_inc(c_hi_ok, 1)
                pool.wait_ge(c_hi_ok, m * 4 + (fb + 1))
                G_.tensor_tensor(out=cT_lo[:, fb, :], in0=c_raw[:, fb % 2, :], in1=cT_hi[:, fb, :].bitcast(F32),
                                 op=ALU.subtract).then_inc(c_done, 1)

            def inverse_root(m):
                pool.wait_ge(ve_ok, m + 1)
                G_.tensor_tensor(out=rstd[:], in0=ve[:], in1=nhalf[:], op=ALU.pow).then_inc(rstd_ok, 1)

            def expand(it, g):
                pool.wait_ge(recip_ok, it.b * NG + (g + 1))
                pool.wait_ge(oT_done, it.b * NG + (g + 1))
                pool.sem_inc(carriers, 1)
                G_.tensor_copy(rT[:].rearrange("p (c r d) -> p c r d", c=4, r=4), recips[:, g % 2, :].rearrange("p (c r) -> p c r", c=4).unsqueeze(3)
                               .to_broadcast([P, 4, 4, HD])).then_inc(rexp_ok, 1)

            def o_low(it, g):
                pool.wait_ge(oT_hi_ok, it.b * NG + (g + 1))
                G_.tensor_tensor(out=oT_lo[:, g % NG, :], in0=rT[:], in1=oT_hi[:, g % NG, :].bitcast(F32),
                                 op=ALU.subtract).then_inc(oT_done, 1)

            pool.sem_inc(oT_done, 1)
            G_.memset(ident[:], 1.0).then_inc(ready, 1)
            G_.memset(mask[:], 0.0).then_inc(ready, 1)
            G_.memset(nhalf[:], -0.5).then_inc(ready, 1)
            pool.wait_ge(ready, 3)
            G_.affine_select(out=ident[:], in_=ident[:], compare_op=ALU.is_equal, fill=0.0, base=0,
                             pattern=[[-1, P]], channel_multiplier=1).then_inc(consts, 1)
            G_.affine_select(out=mask[:, 384:512], in_=mask[:, 384:512], compare_op=ALU.is_ge, fill=MASKED, base=0,
                             pattern=[[-1, P]], channel_multiplier=1).then_inc(consts, 1)
            inverse_root(0)
            for fb in range(4):
                split_context(0, fb)

            def body(it):
                if not it.first:
                    expand(it, -1)
                    o_low(it, -1)
                if it.tail:
                    return
                expand(it, 0)
                o_low(it, 0)
                expand(it, 1)
                if not it.last:
                    inverse_root(it.b + 1)
                o_low(it, 1)
                if not it.last:
                    pool.wait_ge(dense, it.done("V3b", 2))
                    for fb in range(3):
                        split_context(it.b + 1, fb)
                expand(it, 2)
                if not it.last:
                    split_context(it.b + 1, 3)
                o_low(it, 2)
                pool.wait_ge(res_in, it.b * 16 + 16)
                for t in range(QT):
                    G_.tensor_tensor(out=xt[:, t, :], in0=xt[:, t, :], in1=bo_row[:],
                                     op=ALU.add).then_inc(res_ok, 1)

            over_batches(pool, body)


def stage_b(nc, x1, w1, w2, vecs, b2, out):
    B, S, D = x1.shape
    F = w1.shape[1]
    KT = D // P
    FT = F // P
    QT = S // P
    WC = F // 512
    FC = FT // WC
    RING_H = 4

    with ExitStack() as ctx:
        def sb(name, shape, dt=F32):
            return ctx.enter_context(nc.sbuf_tensor(name, shape, dt))

        def pb(name):
            return ctx.enter_context(nc.psum_tensor(name, [P, 512], F32))

        def sem(name):
            return ctx.enter_context(nc.semaphore(name))

        w1_hi = sb("w1_hi", [P, KT, F], F32R)
        w1_lo = sb("w1_lo", [P, KT, F], F32R)
        w2_hi = sb("w2_hi", [P, FT, D], F32R)
        w2_lo = sb("w2_lo", [P, FT, D], F32R)
        raw = sb("raw", [P, 2, KT, 512])
        vec = sb("vecb", [P, 2 * KT + FT])
        b1s = sb("b1s", [P, FT])
        b2_row = sb("b2_row", [P, D])
        xn = sb("xn", [P, QT, D])
        xr = sb("xr", [P, QT, D])
        hT_hi = sb("hT_hi", [P, KT, S], F32R)
        hT_lo = sb("hT_lo", [P, KT, S], F32R)
        g_sb = sb("g_sb", [P, 2, S])
        g_hi = sb("g_hi", [P, RING_H, S], F32R)
        g_lo = sb("g_lo", [P, RING_H, S], F32R)
        ident = sb("identb", [P, P])
        stats = sb("statsb", [P, QT, 6])
        mv = sb("mvb", [P, QT, 2])
        ve = sb("veb", [P, QT])
        rstd = sb("rstdb", [P, QT])
        nhalf = sb("nhalfb", [P, QT])

        bank_f = [pb(f"bank_f{i}") for i in range(2)]
        bank_x = [pb(f"bank_x{i}") for i in range(2)]
        bank_o = [pb(f"bank_o{i}") for i in range(4)]

        carriers = sem("carriersb")
        vec_in, b2_in = sem("vecb_in"), sem("b2_in")
        raw_in = [sem(f"rawb_in{i}") for i in range(2)]
        xn_in, xr_in, stored = sem("xn_in"), sem("xr_in"), sem("out_stored")
        ready, consts, b1_mm, b1_ok, scaled = (sem(n) for n in ("readyb", "constsb", "b1_mm", "b1_ok", "scaledb"))
        w1_hi_ok, w1_ok, w2_hi_ok, w2_ok = (sem(n) for n in ("w1_hi_ok", "w1_ok", "w2_hi_ok", "w2_ok"))
        bn_ok, mv_ok, ve_ok, rstd_ok, xn_ok = (sem(n) for n in ("bnb_ok", "mvb_ok", "veb_ok", "rstdb_ok", "xnb_ok"))
        x_t, hT_hi_ok, hT_ok = (sem(n) for n in ("x_t", "hT_hi_ok", "hT_ok"))
        ffn1, gelu, g_hi_ok, g_ok, ffn2, summed, xr_ok = (
            sem(n) for n in ("ffn1", "gelu", "g_hi_ok", "g_ok", "ffn2", "summed", "xr_ok"))

        x_v = x1.rearrange("b (t p) d -> b p t d", p=P)
        out_v = out.rearrange("b (t p) d -> b p t d", p=P)
        w1_v = w1.rearrange("(t p) f -> p t f", p=P)
        w2_v = w2.rearrange("(c t p) d -> c p t d", p=P, t=FC)

        def over_chunks(eng, body):
            if B > 1:
                with eng.Fori(0, B - 1) as c:
                    body(c, False)
            body(B - 1, True)

        block = ctx.enter_context(nc.Block())

        @block.sync
        def _(sp):
            def one(view, b):
                return view[bass.ds(b, 1)].rearrange("o p t d -> p (o t) d")

            sp.sem_inc(stored, 16)
            sp.dma_start(xn[:], one(x_v, 0)).then_inc(xn_in, 16)
            sp.dma_start(vec[:], vecs).then_inc(vec_in, 16)
            sp.dma_start(b2_row[:], b2.partition_broadcast(P)).then_inc(b2_in, 16)
            for wc in range(WC):
                if wc > 0:
                    sp.wait_ge(w1_ok, wc)
                sp.dma_start(raw[:, 0, :, :], w1_v[:, :, 512 * wc:512 * wc + 512]).then_inc(raw_in[0], 16)
                if wc > 0:
                    sp.wait_ge(w2_ok, wc)
                sp.dma_start(raw[:, 1, :, :], w2_v[wc]).then_inc(raw_in[1], 16)

            def body(c, last):
                sp.wait_ge(stored, c * 64 + 16)
                sp.dma_start(xr[:], one(x_v, c)).then_inc(xr_in, 16)
                if not last:
                    sp.wait_ge(x_t, c * QT + QT)
                    sp.dma_start(xn[:], one(x_v, c + 1)).then_inc(xn_in, 16)
                for t in range(QT):
                    sp.wait_ge(summed, c * QT + (t + 5))
                    sp.dma_start(one(out_v, c)[:, t, :], xr[:, t, :]).then_inc(stored, 16)

            over_chunks(sp, body)
            sp.wait_ge(stored, 64 * B + 16)

        @block.tensor
        def _(pe):
            def split_product(o, lh, ll, rh, rl, first, last):
                pe.matmul(o, lh, rh, start=first, stop=False)
                pe.matmul(o, lh, rl, start=False, stop=False)
                return pe.matmul(o, ll, rh, start=False, stop=last)

            def x_transpose(m, t):
                pe.wait_ge(xn_ok, m * QT + (t + 1))
                pe.wait_ge(hT_ok, m * QT + (t + 1))
                for f in range(KT):
                    mm = pe.transpose(bank_x[t % 2][:, P * f:P * f + P], xn[:, t, P * f:P * f + P], ident[:])
                mm.then_inc(x_t, 1)

            def hidden(c, f):
                if f % FC == 0:
                    pe.wait_ge(w1_ok, f // FC + 1)
                if f == 0:
                    pe.wait_ge(hT_ok, c * QT + (QT + 2))
                pe.wait_ge(gelu, c * FT + (f + 1))
                cols = slice(P * f, P * f + P)
                for kt in range(KT):
                    mm = split_product(bank_f[f % 2][:], w1_hi[:, kt, cols], w1_lo[:, kt, cols],
                                       hT_hi[:, kt, :], hT_lo[:, kt, :], kt == 0, kt == KT - 1)
                mm.then_inc(ffn1, 1)

            def output(c, f):
                if f % FC == 0:
                    pe.wait_ge(w2_ok, f // FC + 1)
                pe.wait_ge(g_ok, c * FT + (f + 3))
                for t in range(QT):
                    if f == 0:
                        pe.wait_ge(summed, c * QT + (t + 1))
                    cols = slice(P * t, P * t + P)
                    mm = split_product(bank_o[t][:], g_hi[:, f % RING_H, cols], g_lo[:, f % RING_H, cols],
                                       w2_hi[:, f, :], w2_lo[:, f, :], f == 0, f == FT - 1)
                mm.then_inc(ffn2, 1)

            pe.sem_inc(ffn2, RING_H)
            pe.wait_ge(vec_in, 16)
            pe.wait_ge(consts, 1)
            for t in range(QT):
                x_transpose(0, t)
            for wc in range(WC):
                pe.wait_ge(raw_in[0], 16 * (wc + 1))
                for f in range(FC * wc, FC * wc + FC):
                    for kt in range(KT):
                        at = P * (f - FC * wc)
                        mm = pe.matmul(bank_o[0][:, f:f + 1], raw[:, 0, kt, at:at + P], vec[:, KT + kt:KT + kt + 1],
                                       start=(kt == 0), stop=(kt == KT - 1))
                mm.then_inc(b1_mm, 1)
            pe.wait_ge(b1_ok, WC)

            def body(c, last):
                for f in range(FT):
                    hidden(c, f)
                    if f >= 2:
                        output(c, f - 2)
                for half in range(2):
                    if not last:
                        x_transpose(c + 1, 2 * half)
                        x_transpose(c + 1, 2 * half + 1)
                    output(c, FT - 2 + half)

            over_chunks(pe, body)

        @block.vector
        def _(dve):
            V = nc.vector

            def layer_norm_stats(m):
                dve.wait_ge(xn_in, m * 16 + 16)
                for t in range(QT):
                    V.bn_stats(stats[:, t, :], xn[:, t, :]).then_inc(bn_ok, 1)
                for t in range(QT):
                    dve.wait_ge(bn_ok, m * QT + (t + 1))
                    dve.sem_inc(carriers, 1)
                    V.bn_aggr(mv[:, t, :], stats[:, t, :]).then_inc(mv_ok, 1)
                dve.wait_ge(mv_ok, m * QT + QT)
                V.tensor_scalar(ve[:], mv[:, :, 1], EPS, None, ALU.add).then_inc(ve_ok, 1)

            def normalise(m, t):
                if t == 0:
                    dve.wait_ge(rstd_ok, m + 1)
                V.tensor_scalar(xn[:, t, :], xn[:, t, :], mv[:, t, 0:1], rstd[:, t:t + 1],
                                ALU.subtract, ALU.mult).then_inc(xn_ok, 1)

            def x_low(m, t):
                dve.wait_ge(hT_hi_ok, m * QT + (t + 1))
                cols = slice(P * t, P * t + P)
                V.tensor_tensor(hT_lo[:, :, cols], bank_x[t % 2][:].rearrange("p (f c) -> p f c", f=KT),
                                hT_hi[:, :, cols].bitcast(F32), ALU.subtract).then_inc(hT_ok, 1)

            def split_gelu(c, f):
                dve.wait_ge(gelu, c * FT + (f + 3))
                dve.wait_ge(ffn2, c * FT + (f + 1))
                V.tensor_copy(g_hi[:, f % RING_H, :], g_sb[:, f % 2, :]).then_inc(g_hi_ok, 1)
                dve.wait_ge(g_hi_ok, c * FT + (f + 1))
                V.tensor_tensor(g_lo[:, f % RING_H, :], g_sb[:, f % 2, :], g_hi[:, f % RING_H, :].bitcast(F32),
                                ALU.subtract).then_inc(g_ok, 1)

            dve.sem_inc(hT_ok, 2)
            dve.sem_inc(g_ok, 2)
            dve.sem_inc(summed, QT)
            layer_norm_stats(0)
            for t in range(QT):
                normalise(0, t)
            for t in range(QT):
                x_low(0, t)
            dve.wait_ge(vec_in, 16)
            for wc in range(WC):
                dve.wait_ge(b1_mm, wc + 1)
                cols = slice(FC * wc, FC * wc + FC)
                V.tensor_tensor(b1s[:, cols], bank_o[0][:, cols], vec[:, 2 * KT + FC * wc:2 * KT + FC * wc + FC],
                                ALU.add).then_inc(b1_ok, 1)
                for kt in range(KT):
                    V.tensor_scalar(raw[:, 0, kt, :], raw[:, 0, kt, :], vec[:, kt:kt + 1], None,
                                    ALU.mult).then_inc(scaled, 1)
                dve.wait_ge(w1_hi_ok, wc + 1)
                fs = slice(512 * wc, 512 * wc + 512)
                V.tensor_tensor(w1_lo[:, :, fs], raw[:, 0, :, :], w1_hi[:, :, fs].bitcast(F32),
                                ALU.subtract).then_inc(w1_ok, 1)
                dve.wait_ge(w2_hi_ok, wc + 1)
                V.tensor_tensor(w2_lo[:, cols, :], raw[:, 1, :, :], w2_hi[:, cols, :].bitcast(F32),
                                ALU.subtract).then_inc(w2_ok, 1)

            def body(c, last):
                for f in range(FT):
                    split_gelu(c, f)
                    if not last:
                        if f == 2:
                            layer_norm_stats(c + 1)
                        if f in (5, 6, 7, 8):
                            normalise(c + 1, f - 5)
                if not last:
                    for t in range(QT):
                        x_low(c + 1, t)
                dve.wait_ge(ffn2, c * FT + (FT + RING_H))
                for t in range(QT):
                    dve.wait_ge(xr_ok, c * QT + (t + 1))
                    V.tensor_tensor(xr[:, t, :], bank_o[t][:], xr[:, t, :], ALU.add).then_inc(summed, 1)

            over_chunks(dve, body)

        @block.scalar
        def _(act):
            A = nc.scalar

            def x_high(m, t):
                act.wait_ge(x_t, m * QT + (t + 1))
                A.copy(hT_hi[:, :, P * t:P * t + P],
                       bank_x[t % 2][:].rearrange("p (f c) -> p f c", f=KT)).then_inc(hT_hi_ok, 1)

            act.sem_inc(gelu, 2)
            for t in range(QT):
                x_high(0, t)
            for wc in range(WC):
                fs = slice(512 * wc, 512 * wc + 512)
                act.wait_ge(scaled, KT * (wc + 1))
                A.copy(w1_hi[:, :, fs], raw[:, 0, :, :]).then_inc(w1_hi_ok, 1)
                act.wait_ge(raw_in[1], 16 * (wc + 1))
                A.copy(w2_hi[:, FC * wc:FC * wc + FC, :], raw[:, 1, :, :]).then_inc(w2_hi_ok, 1)

            def body(c, last):
                for f in range(FT):
                    act.wait_ge(ffn1, c * FT + (f + 1))
                    act.wait_ge(g_ok, c * FT + (f + 1))
                    A.activation(g_sb[:, f % 2, :], bank_f[f % 2][:], ACT.Gelu, bias=b1s[:, f:f + 1],
                                 scale=1.0).then_inc(gelu, 1)
                if not last:
                    for t in range(QT):
                        x_high(c + 1, t)

            over_chunks(act, body)

        @block.gpsimd
        def _(pool):
            G_ = nc.gpsimd

            def inverse_root(m):
                pool.wait_ge(ve_ok, m + 1)
                G_.tensor_tensor(out=rstd[:], in0=ve[:], in1=nhalf[:], op=ALU.pow).then_inc(rstd_ok, 1)

            G_.memset(ident[:], 1.0).then_inc(ready, 1)
            G_.memset(nhalf[:], -0.5).then_inc(ready, 1)
            pool.wait_ge(ready, 2)
            G_.affine_select(out=ident[:], in_=ident[:], compare_op=ALU.is_equal, fill=0.0, base=0,
                             pattern=[[-1, P]], channel_multiplier=1).then_inc(consts, 1)
            inverse_root(0)
            pool.wait_ge(b2_in, 16)

            def body(c, last):
                pool.wait_ge(xr_in, c * 16 + 16)
                for t in range(QT):
                    G_.tensor_tensor(out=xr[:, t, :], in0=xr[:, t, :], in1=b2_row[:], op=ALU.add).then_inc(xr_ok, 1)
                if not last:
                    inverse_root(c + 1)

            over_chunks(pool, body)


def build(nc, x, ctxT, wq, wk, wv, wo, vecs_a, bo, w1, w2, vecs_b, b2, out):
    x1 = nc.dram_tensor("x1_scratch", tuple(x.shape), F32).ap()
    stage_a(nc, x, ctxT, wq, wk, wv, wo, vecs_a, bo, x1)
    stage_b(nc, x1, w1, w2, vecs_b, b2, out)


def kernel(x, ctx_1024, **w):
    import numpy as np
    import concourse.bacc as bacc
    from concourse.bass_utils import run_bass_kernel_spmd

    w = {k.replace("L0_xattn_", ""): np.asarray(v) for k, v in w.items()}
    D = x.shape[-1]

    def by_columns(v):
        return np.asarray(v).reshape(-1, P).T

    def feature_major(v):
        return v.reshape(*v.shape[:-1], HEADS // 4, 4, D // HEADS).swapaxes(-1, -2).reshape(v.shape)

    arrays = {
        "x": np.asarray(x),
        "ctxT": np.asarray(ctx_1024).transpose(0, 2, 1),
        "wq": feature_major(w["wq"]),
        "wk": feature_major(w["wk"]),
        "wv": w["wv"],
        "wo": w["wo"],
        "vecs_a": np.stack([by_columns(v) for v in (w["ln1_g"], w["ln1_b"], feature_major(w["bq"]),
                                                    feature_major(w["bk"]), w["bv"])], axis=1),
        "bo": w["bo"],
        "w1": w["w1"],
        "w2": w["w2"],
        "vecs_b": np.concatenate([by_columns(w["ln2_g"]), by_columns(w["ln2_b"]), by_columns(w["b1"])], axis=1),
        "b2": w["b2"],
    }
    nc = bacc.Bacc("TRN2", target_bir_lowering=False, num_devices=1)
    arrays = {f"in_{k}": np.ascontiguousarray(v) for k, v in arrays.items()}
    args = [nc.dram_tensor(k, v.shape, mybir.dt.from_np(v.dtype), kind="ExternalInput").ap()
            for k, v in arrays.items()]
    out = nc.dram_tensor("out", x.shape, F32, kind="ExternalOutput").ap()
    build(nc, *args, out)
    r = run_bass_kernel_spmd(nc, [arrays], core_ids=[0])
    return r.results[0]["out"]
```

```python
from contextlib import ExitStack

import concourse.bass as bass
from concourse import mybir
from concourse.alu_op_type import AluOpType as ALU

ACT = mybir.ActivationFunctionType
F32 = mybir.dt.float32
F32R = mybir.dt.float32r
BF16 = mybir.dt.bfloat16

P = 128
EPS = 1e-5
MASKED = 3.0e38

HEADS = 16
BANKS_S = 2
BANKS_D = 3
SLOTS_S = 4
LAG = 3
POS = [0, 1, 3, 2]


def tile_of(k):
    if k < 4:
        return 0, k, (0, 1)
    return 1, (k - 4) // 2, (2 + (k - 4) % 2,)


ACT_MOVES = (5, 9, 11)


def act_moves(k):
    return k in ACT_MOVES


def stage_a(nc, x, ctxT, wq, wk, wv, wo, vecs, bo, x1):
    B, S, D = x.shape
    HD = D // HEADS
    KT = D // P
    QT = S // P
    NG = HEADS // 4
    TG = 12
    TB = NG * TG
    SCALE = float(HD) ** -0.5
    HALF = D // 2

    COUNT = {"X": 4, "Q": 12, "K": 12, "V": 24, "R": 4, "O": 12, "B": 4}
    PRO = ["X0", "X1", "X2", "X3", "Q0", "K0", "V0a"]
    BESIDE = [
        [("B", {0: 4}), ("Q1", {0: 4, 1: 4, 2: 4}), ("K1", {2: 4, 3: 4, 4: 4}), ("R", {5: 4}),
         ("V1a", {6: 8, 7: 8, 8: 8}), ("O0", {10: 6, 11: 6})],
        [("Q2", {0: 6, 1: 6}), ("K2", {2: 4, 3: 4, 4: 4}), ("R", {4: 4}), ("O1", {5: 12}), ("O2", {7: 12}),
         ("O3", {8: 6, 9: 6}), ("V0b", {10: 12, 11: 12})],
        [("Q3", {0: 4, 1: 4, 2: 4}), ("K3", {2: 4, 3: 4, 4: 4}), ("R", {4: 4}), ("V1b", {5: 12, 6: 12}),
         ("X0", {8: 4}), ("X1", {8: 4}), ("X2", {9: 4}), ("X3", {10: 4})],
        [("Q0", {1: 6, 2: 6}), ("K0", {3: 6, 4: 6}), ("R", {4: 4}), ("V0a", {6: 8, 7: 4, 8: 4, 9: 4, 10: 4})],
    ]
    TAIL = [("R", {5: 4}), ("O0", {8: 12}), ("O1", {9: 12}), ("O2", {10: 12}), ("O3", {11: 12})]
    R_AT, PV1_AT, PV0_AT, O_PROD_AT, O_HIGH_AT, O_HIGH_LATE = 4, 5, 9, 6, 7, 10
    CONTEXT_AT = (2 * TG + 8, 2 * TG + 9, 2 * TG + 11, 3 * TG + 1)
    STATS_AT, NORMALISE_AT = (1, 3, 4, 4), (5, 6, 6, 7)

    def beside(groups, first, last):
        steps = [[] for _ in range(TG * len(groups))]
        for g, jobs in enumerate(groups):
            for job, at in jobs:
                if job == "R" and first and g == 0 or job == "B" and not first or job[0] == "O" and first:
                    continue
                if last and (job[0] == "X" or job in ("Q0", "K0", "V0a")):
                    continue
                done = 0
                for k, n in at.items():
                    steps[TG * g + k].append((job, done, done + n))
                    done += n
                assert done == COUNT[job[0]]
        return steps

    assert B > 2

    with ExitStack() as ctx:
        def sb(name, shape, dt=F32):
            return ctx.enter_context(nc.sbuf_tensor(name, shape, dt))

        def pb(name):
            return ctx.enter_context(nc.psum_tensor(name, [P, 512], F32))

        def sem(name):
            return ctx.enter_context(nc.semaphore(name))

        w_hi = [sb(f"{n}_hi", [P, KT, D], F32R) for n in ("wq", "wk", "wv", "wo")]
        w_lo = [sb(f"{n}_lo", [P, KT, D], F32R) for n in ("wq", "wk", "wv", "wo")]
        vec = sb("vec", [P, 5, 4])
        bqs = sb("bqs", [P, NG])
        bo_row = sb("bo_row", [P, D])
        xt = sb("xt", [P, QT, D])
        xnT_hi = sb("xnT_hi", [P, KT, S], F32R)
        xnT_lo = sb("xnT_lo", [P, KT, S], F32R)
        c_raw = sb("c_raw", [P, 2, S])
        cT_hi = sb("cT_hi", [P, KT, S], F32R)
        cT_lo = sb("cT_lo", [P, KT, S], F32R)
        st_hi = sb("st_hi", [P, 2, S], F32R)
        st_lo = sb("st_lo", [P, 2, S], F32R)
        stack = sb("stack", [P, 2, 2, 4, S], F32R)
        v_sb = sb("v_sb", [P, QT, D])
        sm = sb("sm", [P, SLOTS_S, 512])
        pT = sb("pT", [P, 4, 1280])
        rT = sb("rT", [P, 512])
        oT_hi = sb("oT_hi", [P, NG, S], F32R)
        oT_lo = sb("oT_lo", [P, NG, S], F32R)
        mask = sb("mask", [P, 512], BF16)
        ident = sb("ident", [P, P])
        mins = sb("mins", [P, 2, 16])
        sums = sb("sums", [P, 2, 16])
        recips = sb("recips", [P, 2, 16])
        stats = sb("stats", [P, QT, 6])
        mv = sb("mv", [P, QT, 2])
        ve = sb("ve", [P, QT])
        rstd = sb("rstd", [P, QT])
        nhalf = sb("nhalf", [P, QT])
        pT_flat = pT[:].rearrange("p a b -> p (a b)")
        raw = [pT_flat[:, 0:KT * D], pT_flat[:, KT * D:2 * KT * D], sm[:].rearrange("p t n -> p (t n)"),
               pT_flat[:, 0:KT * D]]
        assert SLOTS_S * 512 == KT * D
        wq_scaled = v_sb[:].rearrange("p t n -> p (t n)")
        bvx = rT[:].rearrange("p (t m) -> p t m", t=KT)

        bank_s = [pb(f"bank_s{i}") for i in range(BANKS_S)]
        bank_t = [pb(f"bank_t{i}") for i in range(2)]
        bank_v = pb("bank_v")
        bank_d = [pb(f"bank_d{i}") for i in range(BANKS_D)]

        vec_in, bo_in = sem("vec_in"), sem("bo_in")
        raw_in = [sem(f"raw_in{i}") for i in range(4)]
        x_in, res_in, stored = sem("x_in"), sem("res_in"), sem("stored")
        c_in = [sem(f"c_in{i}") for i in range(2)]
        stacked = sem("stacked")
        carriers = sem("carriers")
        ready = sem("ready")
        consts, bias_mm, scaled, w_hi_done, w_lo_done, wo_lo_done, bvx_ok, bias_ok = (
            sem(n) for n in ("consts", "bias_mm", "scaled", "w_hi_done", "w_lo_done", "wo_lo_done", "bvx_ok",
                             "bias_ok"))
        scored, masked, probs, transposed, pv_done = (
            sem(n) for n in ("scored", "masked", "probs", "transposed", "pv_done"))
        moved = [sem(f"moved{i}") for i in range(2)]
        recip_ok, rexp_ok, o_prod, oT_hi_ok, oT_done = (
            sem(n) for n in ("recip_ok", "rexp_ok", "o_prod", "oT_hi_ok", "oT_done"))
        dense = sem("dense")
        d_free = [sem(f"d_free{i}") for i in range(BANKS_D)]
        qk_hi, x_hi = sem("qk_hi"), sem("x_hi")
        bn_ok, mv_ok, ve_ok, rstd_ok, xn_ok, c_hi_ok, c_done, res_ok = (
            sem(n) for n in ("bn_ok", "mv_ok", "ve_ok", "rstd_ok", "xn_ok", "c_hi_ok", "c_done", "res_ok"))

        def jobs_of(steps):
            order, ends = [], {}
            for n, slot in enumerate(steps):
                for job, first, _ in slot:
                    if first == 0:
                        order.append((job, n // TG))
                    ends[job, n // TG] = n
            return order, ends

        class Iteration:
            def __init__(self, b, start, steps, per_batch=0, first=False, last=False, tail=False):
                self.b, self.start, self.steps, self.per_batch = b, start, steps, per_batch
                self.first, self.last, self.tail = first, last, tail
                self.order, self.ends = jobs_of(steps)
            def place(self, job, g):
                if g < 0:
                    return {"V0a": -1}[job]
                return self.order.index((job, g))
            def bank(self, job, g):
                return (self.start + self.place(job, g)) % BANKS_D
            def done(self, job, g):
                return self.b * self.per_batch + (self.start + self.place(job, g) + 1)
            def bank_wait(self, job, g):
                return self.b * (self.per_batch // BANKS_D) + ((self.start + self.place(job, g)) // BANKS_D + 1)
            def bank_read(self, job, g):
                return self.b * (self.per_batch // BANKS_D) + ((self.start + self.place(job, g)) // BANKS_D + 2)
            def ended(self, n):
                return [job for job, at in self.ends.items() if at == n]

        def count(steps):
            return len(jobs_of(steps)[0])

        pro = Iteration(0, 0, [[(job, 0, COUNT[job[0]])] for job in PRO], first=True)
        first_plan, mid_plan, last_plan = (
            beside(BESIDE, *ends) for ends in ((True, False), (False, False), (False, True)))
        PER = count(mid_plan)
        assert PER % BANKS_D == 0
        mid_start = len(PRO) + count(first_plan)

        def over_batches(eng, body):
            body(Iteration(0, len(PRO), first_plan, first=True))
            with eng.Fori(1, B - 1) as b:
                body(Iteration(b, mid_start - PER, mid_plan, per_batch=PER))
            last_start = mid_start + (B - 2) * PER
            body(Iteration(B - 1, last_start, last_plan, last=True))
            body(Iteration(B, last_start + count(last_plan), beside([TAIL], False, False), tail=True))

        x_v = x.rearrange("b (t p) d -> b p t d", p=P)
        x1_v = x1.rearrange("b (t p) d -> b p t d", p=P)
        c_v = ctxT.rearrange("b (t p) s -> b p t s", p=P)

        block = ctx.enter_context(nc.Block())

        @block.sync
        def _(sp):
            def one(view, b):
                return view[bass.ds(b, 1)].rearrange("o p t d -> p (o t) d")

            def load_c(m, fb):
                sp.dma_start(c_raw[:, fb % 2, :], one(c_v, m)[:, fb, :]).then_inc(c_in[fb % 2], 16)

            def stack_parts(it, w, job, g, par):
                sp.wait_ge(d_free[it.bank(job, g)], it.bank_read(job, g))
                for part, src in enumerate(((st_hi, st_hi, st_lo, st_lo), (st_hi, st_lo, st_hi, st_lo))[w]):
                    sp.dma_start(stack[32 * part:32 * part + 32, par, w, :, :].bitcast(F32),
                                 src[:, w, :].bitcast(F32)).then_inc(stacked, 16)

            sp.sem_inc(stored, 16)
            sp.dma_start(vec[:], vecs).then_inc(vec_in, 16)
            sp.dma_start(xt[:], one(x_v, 0)).then_inc(x_in, 16)

            def load_weight(i):
                sp.dma_start(raw[i].rearrange("p (t n) -> p t n", t=KT),
                             (wq, wk, wv, wo)[i].rearrange("(t p) n -> p t n", p=P)).then_inc(raw_in[i], 16)

            load_weight(0)
            load_c(0, 0)
            load_c(0, 1)
            load_weight(1)
            load_weight(2)
            sp.dma_start(bo_row[:], bo.partition_broadcast(P)).then_inc(bo_in, 16)
            sp.wait_ge(c_done, 1)
            load_c(0, 2)
            sp.wait_ge(c_done, 2)
            load_c(0, 3)
            sp.wait_ge(scaled, KT)
            sp.wait_ge(bias_mm, 1)
            load_weight(3)
            for w, job in enumerate(("Q0", "K0")):
                stack_parts(pro, w, job, 0, 0)

            def stacks(it, g):
                if g > 0:
                    sp.wait_ge(scored, it.b * TB + TG * g)
                    sp.sem_inc(carriers, 1)
                elif not it.first:
                    sp.wait_ge(scored, it.b * TB)
                    sp.sem_inc(carriers, 1)
                for w, name in enumerate("QK"):
                    stack_parts(it, w, f"{name}{(g + 1) % NG}", g, (g + 1) % 2)

            def store(it, t):
                g = 0 if it.tail or t == 0 else 1
                sp.wait_ge(d_free[it.bank(f"O{t}", g)], it.bank_read(f"O{t}", g))
                sp.dma_start(one(x1_v, it.b - 1)[:, t, :], xt[:, t, :]).then_inc(stored, 16)

            def body(it):
                b = it.b
                if it.tail:
                    for t in range(QT):
                        store(it, t)
                    return
                if not it.last:
                    sp.wait_ge(c_done, b * 4 + 4)
                    load_c(b + 1, 0)
                    load_c(b + 1, 1)
                for g in range(2):
                    stacks(it, g)
                    if not it.first:
                        for t in ((0,), (1, 2, 3))[g]:
                            store(it, t)
                if it.first:
                    sp.wait_ge(dense, pro.done("X3", 0))
                else:
                    sp.wait_ge(stored, b * 64 + 16)
                if not it.last:
                    sp.dma_start(xt[:], one(x_v, b + 1)).then_inc(x_in, 16)
                stacks(it, 2)
                if not it.last:
                    sp.wait_ge(c_done, b * 4 + 5)
                    load_c(b + 1, 2)
                    sp.wait_ge(c_done, b * 4 + 6)
                    load_c(b + 1, 3)
                    sp.wait_ge(dense, it.done("X3", 2))
                sp.dma_start(xt[:], one(x_v, b)).then_inc(res_in, 16)
                if not it.last:
                    stacks(it, 3)

            over_batches(sp, body)
            sp.wait_ge(stored, 64 * B + 16)

        @block.tensor
        def _(pe):
            def dense_step(it, job, g, i, j):
                kind, bank = job[0], bank_d[it.bank(job, g)]
                if i == 0:
                    pe.wait_ge(d_free[it.bank(job, g)], it.bank_wait(job, g))
                if kind == "X":
                    t, m = int(job[1]), (0 if it is pro else it.b + 1)
                    pe.wait_ge(xn_ok, m * QT + (t + 1))
                    for f in range(KT):
                        mm = pe.transpose(bank[:, P * f:P * f + P], xt[:, t, P * f:P * f + P], ident[:])
                elif kind == "B":
                    pe.wait_ge(bvx_ok, 1)
                    pe.wait_ge(raw_in[3], 16)
                    for kt in range(KT):
                        mm = pe.matmul(bank[:], bvx[:, kt, :], raw[3][:, D * kt:D * kt + D],
                                       start=(kt == 0), stop=(kt == KT - 1))
                elif kind == "R":
                    pe.wait_ge(rexp_ok, it.b * NG + g)
                    for c in range(QT):
                        mm = pe.transpose(bank[:, P * c:P * c + P],
                                          rT[:, P * c:P * c + P], ident[:])
                else:
                    t = int(job[1])
                    if i == 0 and job == "O0" and not it.tail:
                        pe.wait_ge(wo_lo_done, 1)
                    if i == 0 and job == "O0":
                        pe.wait_ge(oT_done, it.b * NG + 1)
                    if i == 0 and job == "Q0":
                        for m in range(QT - BANKS_D, QT):
                            x, xg = f"X{m}", 0 if it is pro else 2
                            pe.wait_ge(d_free[it.bank(x, xg)], it.bank_read(x, xg))
                    for n in range(i, j):
                        tile, at = divmod(n, 12)
                        kt, part = divmod(at, 3)
                        if job == "K0" and part == 0:
                            pe.wait_ge(c_done, (0 if it is pro else it.b * 4 + 4) + (kt + 1))
                        cols, out = slice(P * t, P * t + P), bank[:]
                        if kind == "Q":
                            left, right, rows = w_of[0], xnT, slice(0, S)
                        elif kind == "K":
                            left, right, rows = w_of[1], cT, slice(0, S)
                        elif kind == "V":
                            left, right = cT, w_of[2]
                            cols = slice(P * (2 * t + tile), P * (2 * t + tile) + P)
                            rows = slice(HALF * "ab".index(job[2]), HALF * "ab".index(job[2]) + HALF)
                            out = bank[:, HALF * tile:HALF * tile + HALF]
                        else:
                            left, right, rows = oT, w_of[3], slice(0, D)
                            cols = slice(P * POS[t], P * POS[t] + P)
                        mm = pe.matmul(out, left[part // 2][:, kt, cols], right[part % 2][:, kt, rows],
                                       start=(at == 0), stop=(at == 11))
                if j == COUNT[kind]:
                    mm.then_inc(dense, 1)

            def score(it, n):
                g, k = divmod(n, TG)
                _, r, qts = tile_of(k)
                if k == 0:
                    pe.wait_ge(stacked, it.b * (128 * NG) + 128 * (g + 1))
                pe.wait_ge(masked, it.b * TB + (n + 1))
                off = 0
                for qt in qts:
                    w = P * (qt + 1)
                    mm = pe.matmul(bank_s[n % BANKS_S][:, off:off + w], stack[:, g % 2, 0, r, P * qt:P * qt + P],
                                   stack[:, g % 2, 1, r, 0:w], start=True, stop=True)
                    off += w
                mm.then_inc(scored, 1)

            def p_transpose(it, n):
                k = n % TG
                _, r, qts = tile_of(k)
                pe.wait_ge(probs, it.b * TB + (n + 1))
                pe.wait_ge(moved[n % 2], it.b * (TB // 2) + (n // 2 + 1))
                for c in range(sum(qt + 1 for qt in qts)):
                    mm = pe.transpose(bank_t[n % 2][:, P * c:P * c + P], sm[:, n % SLOTS_S, P * c:P * c + P], ident[:])
                mm.then_inc(transposed, 1)

            def pv(it, g, pair):
                last_tile = TG * g + (3 if pair == 0 else 11)
                for i in range(2):
                    pe.wait_ge(moved[i], it.b * (TB // 2) + ((last_tile + 1) // 2 + 1))
                if pair == 0:
                    pe.wait_ge(o_prod, it.b * NG + (g + 1))
                if g in (0, 2):
                    name = f"V{pair}{'ab'[g // 2]}"
                    at = {"V0a": -1, "V1a": 0, "V0b": 1, "V1b": 2}[name]
                    pe.wait_ge(d_free[it.bank(name, at)], it.bank_read(name, at))
                if pair == 0:
                    parts = [(0, 0, 256, 0), (1, 256, 128, 128)]
                else:
                    parts = [(0, 384, 256, 256), (1, 640, 256, 256), (2, 896, 256, 256), (3, 1152, 128, 256)]
                for j, at, w, to in parts:
                    for r in range(4):
                        h = 4 * (g % NG) + r
                        mm = pe.matmul(bank_v[32 * r:32 * r + 32, to:to + w], v_sb[:, j, HD * h:HD * h + HD],
                                       pT[:, r, at:at + w], start=(j == 0), stop=(j == len(parts) - 1),
                                       skip_group_check=True)
                mm.then_inc(pv_done, 1)

            w_of = list(zip(w_hi, w_lo))
            xnT, cT, oT = (xnT_hi, xnT_lo), (cT_hi, cT_lo), (oT_hi, oT_lo)

            pe.sem_inc(transposed, SLOTS_S)
            pe.sem_inc(pv_done, 2)
            pe.wait_ge(consts, 1)
            for job in PRO:
                if job == "Q0":
                    pe.wait_ge(vec_in, 16)
                    pe.wait_ge(raw_in[0], 16)
                    for g in range(NG):
                        for kt in range(KT):
                            mm = pe.matmul(bank_s[0][:, g:g + 1], raw[0][:, D * kt + P * g:D * kt + P * g + P],
                                           vec[:, 1, kt:kt + 1], start=(kt == 0), stop=(kt == KT - 1))
                    mm.then_inc(bias_mm, 1)
                    pe.wait_ge(w_lo_done, 1)
                if job == "K0":
                    pe.wait_ge(w_lo_done, 2)
                if job == "V0a":
                    pe.wait_ge(w_lo_done, 3)
                dense_step(pro, job, 0, 0, COUNT[job[0]])

            def body(it):
                for n, steps in enumerate(it.steps):
                    g, k = divmod(n, TG)
                    if not it.tail:
                        score(it, n)
                    for job, i, j in steps:
                        dense_step(it, job, g, i, j)
                    if k == PV1_AT and not (it.first and g == 0):
                        pv(it, g - 1, 1)
                    if k == PV0_AT and not it.tail:
                        pv(it, g, 0)
                    if n >= LAG and not it.tail or n < LAG and not it.first:
                        p_transpose(it, n - LAG)

            over_batches(pe, body)

        def move_tile(eng, copy, it, n):
            g, k = divmod(n, TG)
            pair, r, qts = tile_of(k)
            eng.wait_ge(transposed, it.b * TB + (n + 1 + SLOTS_S))
            eng.wait_ge(pv_done, it.b * (2 * NG) + (2 * g + pair + 1))
            bank = bank_t[n % 2]
            if pair == 0:
                out, src = pT[:, r, 0:384], bank[:, 0:384]
            else:
                qt = qts[0]
                first = 0 if qt == 3 else P
                out = pT[:, r, 384:1280].rearrange("p (c q) -> p c q", q=P)[:, first // P::2, :]
                src = bank[:, 0:P * (qt + 1)].rearrange("p (c q) -> p c q", q=P)
            copy(out, src).then_inc(moved[n % 2], 1)

        @block.vector
        def _(dve):
            V = nc.vector

            def layer_norm_stats(m, t):
                if t == 0:
                    dve.wait_ge(x_in, m * 16 + 16)
                V.bn_stats(stats[:, t, :], xt[:, t, :]).then_inc(bn_ok, 1)
                if t < QT - 1:
                    return
                for t in range(QT):
                    dve.wait_ge(bn_ok, m * QT + (t + 1))
                    dve.sem_inc(carriers, 1)
                    V.bn_aggr(mv[:, t, :], stats[:, t, :]).then_inc(mv_ok, 1)
                dve.wait_ge(mv_ok, m * QT + QT)
                V.tensor_scalar(ve[:], mv[:, :, 1], EPS, None, ALU.add).then_inc(ve_ok, 1)

            def normalise(m, t):
                if t == 0:
                    dve.wait_ge(rstd_ok, m + 1)
                V.tensor_scalar(xt[:, t, :], xt[:, t, :], mv[:, t, 0:1], rstd[:, t:t + 1],
                                ALU.subtract, ALU.mult).then_inc(xn_ok, 1)

            def context_high(m, fb):
                dve.wait_ge(c_in[fb % 2], m * 32 + 16 * (fb // 2 + 1))
                V.tensor_copy(cT_hi[:, fb, :], c_raw[:, fb % 2, :]).then_inc(c_hi_ok, 1)

            def x_low(it, job, g, m):
                t = int(job[1])
                dve.wait_ge(x_hi, m * QT + (t + 1))
                cols = slice(P * t, P * t + P)
                V.tensor_tensor(xnT_lo[:, :, cols], bank_d[it.bank(job, g)][:].rearrange("p (f c) -> p f c", f=KT),
                                xnT_hi[:, :, cols].bitcast(F32), ALU.subtract).then_inc(d_free[it.bank(job, g)], 1)

            def qk_low(it, job, g, G):
                w, hg, bank = "QK".index(job[0]), int(job[1]), it.bank(job, g)
                dve.wait_ge(qk_hi, G * 2 + (w + 1))
                bias = bqs[:, hg:hg + 1] if w == 0 else vec[:, 3, hg:hg + 1]
                V.scalar_tensor_tensor(st_lo[:, w, :], bank_d[bank][:], bias, st_hi[:, w, :].bitcast(F32),
                                       ALU.add, ALU.subtract).then_inc(d_free[bank], 1)

            def mask_and_max(it, n):
                g, k = divmod(n, TG)
                _, r, qts = tile_of(k)
                dve.wait_ge(scored, it.b * TB + (n + 1))
                dve.wait_ge(transposed, it.b * TB + (n + 1))
                dve.sem_inc(carriers, 1)
                off = 0
                for qt in qts:
                    w = P * (qt + 1)
                    c = 4 * POS[qt] + r
                    op = V.tensor_tensor_reduce(sm[:, n % SLOTS_S, off:off + w], bank_s[n % BANKS_S][:, off:off + w],
                                                mask[:, 512 - w:512], 1.0, 0.0, ALU.add, ALU.min,
                                                mins[:, g % 2, c:c + 1])
                    off += w
                op.then_inc(masked, 1)

            def o_product(it, g):
                dve.wait_ge(d_free[it.bank("R", g + 1)], it.bank_read("R", g + 1))
                dve.wait_ge(pv_done, it.b * (2 * NG) + (2 * g + 4))
                V.tensor_tensor(rT[:], bank_v[:], rT[:], ALU.mult).then_inc(o_prod, 1)

            dve.sem_inc(masked, BANKS_S)
            dve.sem_inc(o_prod, 1)
            for i in range(2):
                dve.sem_inc(moved[i], 1)
            for i in range(BANKS_D):
                dve.sem_inc(d_free[i], 1)
            dve.wait_ge(vec_in, 16)
            V.tensor_copy(bvx, vec[:, 4, :].unsqueeze(2).to_broadcast([P, KT, P])).then_inc(bvx_ok, 1)
            for t in range(QT):
                layer_norm_stats(0, t)
            for fb in range(2):
                context_high(0, fb)
            dve.wait_ge(raw_in[0], 16)
            for kt in range(KT):
                V.tensor_scalar(wq_scaled[:, D * kt:D * kt + D], raw[0][:, D * kt:D * kt + D],
                                vec[:, 0, kt:kt + 1], -SCALE, ALU.mult, ALU.mult).then_inc(scaled, 1)
            for t in range(QT):
                normalise(0, t)

            def weight_low(i, done):
                dve.wait_ge(w_hi_done, i + 1)
                V.tensor_tensor(w_lo[i][:].rearrange("p t n -> p (t n)"), raw[i] if i else wq_scaled,
                                w_hi[i][:].rearrange("p t n -> p (t n)").bitcast(F32),
                                ALU.subtract).then_inc(done, 1)

            weight_low(0, w_lo_done)
            for t in range(QT):
                x_low(pro, f"X{t}", 0, 0)
            for fb in (2, 3):
                context_high(0, fb)
            dve.wait_ge(bias_mm, 1)
            V.tensor_tensor(bqs[:], bank_s[0][:, 0:NG], vec[:, 2, :], ALU.add).then_inc(bias_ok, 1)
            dve.wait_ge(bias_ok, 1)
            V.tensor_scalar(bqs[:], bqs[:], -SCALE, None, ALU.mult).then_inc(scaled, 1)
            weight_low(1, w_lo_done)
            dve.wait_ge(scaled, KT + 1)
            qk_low(pro, "Q0", 0, 0)
            weight_low(2, w_lo_done)
            qk_low(pro, "K0", 0, 0)
            weight_low(3, wo_lo_done)
            dve.wait_ge(consts, 2)

            def body(it):
                for n in range(len(it.steps) + it.tail):
                    g, k = divmod(n, TG)
                    if not it.tail:
                        mask_and_max(it, n)
                    if (n > LAG and not it.tail or n <= LAG and not it.first) and not act_moves((n - LAG - 1) % TG):
                        move_tile(dve, V.tensor_copy, it, n - LAG - 1)
                    beside_previous = g < NG and not (it.first and g == 0) and n < len(it.steps)
                    if k == 1 and beside_previous:
                        dve.wait_ge(probs, it.b * TB + TG * g)
                        V.reciprocal(recips[:, (g - 1) % 2, :], sums[:, (g - 1) % 2, :]).then_inc(recip_ok, 1)
                    if k == O_PROD_AT and beside_previous:
                        o_product(it, g - 1)
                    for fb in range(KT):
                        if n == CONTEXT_AT[fb] and not it.last and not it.tail:
                            if fb == 0:
                                dve.wait_ge(dense, it.done("V1b", 2))
                            context_high(it.b + 1, fb)
                    if not it.last and not it.tail and g == 2:
                        for t in range(QT):
                            if k == STATS_AT[t]:
                                layer_norm_stats(it.b + 1, t)
                        for t in range(QT):
                            if k == NORMALISE_AT[t]:
                                normalise(it.b + 1, t)
                    for job, jg in it.ended(n - 1):
                        if job[0] == "X":
                            x_low(it, job, jg, it.b + 1)
                        if job[0] in "QK":
                            qk_low(it, job, jg, it.b * NG + (jg + 1))
                    for job, jg in it.ended(n):
                        if job == "B":
                            dve.wait_ge(dense, it.done(job, jg))
                            dve.wait_ge(bo_in, 16)
                            V.tensor_tensor(bo_row[:], bank_d[it.bank(job, jg)][:], bo_row[:],
                                            ALU.add).then_inc(d_free[it.bank(job, jg)], 1)
                        if job[0] == "O":
                            t, bank = int(job[1]), it.bank(job, jg)
                            dve.wait_ge(dense, it.done(job, jg))
                            dve.wait_ge(res_ok, it.b * QT + (t + 1 - QT))
                            V.tensor_tensor(xt[:, t, :], bank_d[bank][:], xt[:, t, :],
                                            ALU.add).then_inc(d_free[bank], 1)

            over_batches(dve, body)

        @block.scalar
        def _(act):
            A = nc.scalar

            def x_high(it, job, g):
                t = int(job[1])
                act.wait_ge(dense, it.done(job, g))
                A.copy(xnT_hi[:, :, P * t:P * t + P],
                       bank_d[it.bank(job, g)][:].rearrange("p (f c) -> p f c", f=KT)).then_inc(x_hi, 1)

            def qk_high(it, job, g, G):
                w, hg, bank = "QK".index(job[0]), int(job[1]), it.bank(job, g)
                act.wait_ge(dense, it.done(job, g))
                if it is not pro:
                    act.wait_ge(stacked, G * 128)
                bias = bqs[:, hg:hg + 1] if w == 0 else vec[:, 3, hg:hg + 1]
                A.activation(st_hi[:, w, :], bank_d[bank][:], ACT.Identity, bias=bias,
                             scale=1.0).then_inc(qk_hi, 1)

            def v_copy(it, job, g):
                t, half, bank = int(job[1]), "ab".index(job[2]), it.bank(job, g)
                act.wait_ge(dense, it.done(job, g))
                ahead = 1 if g == NG - 1 else 0
                if not (it.first and not ahead):
                    act.wait_ge(pv_done, it.b * (2 * NG) + (2 * NG * (ahead - 1) + 4 * half + 6))
                A.copy(v_sb[:, 2 * t:2 * t + 2, HALF * half:HALF * half + HALF],
                       bank_d[bank][:].rearrange("p (t c) -> p t c", t=2)).then_inc(d_free[bank], 1)

            def exponential(it, n):
                g, k = divmod(n, TG)
                _, r, qts = tile_of(k)
                act.wait_ge(masked, it.b * TB + (n + 1 + BANKS_S))
                off = 0
                for qt in qts:
                    w = P * (qt + 1)
                    c = 4 * POS[qt] + r
                    row = sm[:, n % SLOTS_S, off:off + w]
                    op = A.activation(row, row, ACT.Exp, bias=mins[:, g % 2, c:c + 1], scale=-1.0,
                                      accum_out=sums[:, g % 2, c:c + 1])
                    off += w
                op.then_inc(probs, 1)

            def r_copy(it, g):
                bank = it.bank("R", g + 1)
                act.wait_ge(dense, it.done("R", g + 1))
                A.copy(rT[:], bank_d[bank][:]).then_inc(d_free[bank], 1)

            def o_high(it, g):
                act.wait_ge(o_prod, it.b * NG + (g + 2))
                if g == 0 and not it.first:
                    act.wait_ge(dense, it.done("O3", 1))
                A.copy(oT_hi[:, g % NG, :], rT[:]).then_inc(oT_hi_ok, 1)

            def weight_high(i):
                act.wait_ge(raw_in[i], 16)
                A.copy(w_hi[i][:].rearrange("p t n -> p (t n)"), raw[i] if i else wq_scaled).then_inc(w_hi_done, 1)

            act.wait_ge(scaled, KT)
            weight_high(0)
            for t in range(QT):
                x_high(pro, f"X{t}", 0)
            weight_high(1)
            act.wait_ge(scaled, KT + 1)
            qk_high(pro, "Q0", 0, 0)
            weight_high(2)
            qk_high(pro, "K0", 0, 0)
            weight_high(3)
            v_copy(pro, "V0a", 0)

            def body(it):
                for n in range(len(it.steps)):
                    g, k = divmod(n, TG)
                    if not it.tail:
                        exponential(it, n)
                    if (n > LAG and not it.tail or n <= LAG and not it.first) and act_moves((n - LAG - 1) % TG):
                        move_tile(act, A.copy, it, n - LAG - 1)
                    if not (it.first and g == 0):
                        if k == R_AT:
                            r_copy(it, g - 1)
                        if k == (O_HIGH_LATE if g == 1 else O_HIGH_AT):
                            o_high(it, g - 1)
                    for job, jg in it.ended(n):
                        if job[0] == "X":
                            x_high(it, job, jg)
                        if job[0] in "QK":
                            qk_high(it, job, jg, it.b * NG + (jg + 1))
                        if job[0] == "V":
                            v_copy(it, job, jg)

            over_batches(act, body)

        @block.gpsimd
        def _(pool):
            G_ = nc.gpsimd

            def context_low(m, fb):
                pool.wait_ge(c_hi_ok, m * 4 + (fb + 1))
                G_.tensor_tensor(out=cT_lo[:, fb, :], in0=c_raw[:, fb % 2, :], in1=cT_hi[:, fb, :].bitcast(F32),
                                 op=ALU.subtract).then_inc(c_done, 1)

            def inverse_root(m):
                pool.wait_ge(ve_ok, m + 1)
                G_.tensor_tensor(out=rstd[:], in0=ve[:], in1=nhalf[:], op=ALU.pow).then_inc(rstd_ok, 1)

            def expand(it, g):
                pool.wait_ge(recip_ok, it.b * NG + (g + 1))
                pool.wait_ge(oT_done, it.b * NG + (g + 1))
                pool.sem_inc(carriers, 1)
                G_.tensor_copy(rT[:].rearrange("p (c r d) -> p c r d", c=4, r=4),
                               recips[:, g % 2, :].rearrange("p (c r) -> p c r", c=4).unsqueeze(3)
                               .to_broadcast([P, 4, 4, HD])).then_inc(rexp_ok, 1)

            def o_low(it, g):
                pool.wait_ge(oT_hi_ok, it.b * NG + (g + 1))
                G_.tensor_tensor(out=oT_lo[:, g % NG, :], in0=rT[:], in1=oT_hi[:, g % NG, :].bitcast(F32),
                                 op=ALU.subtract).then_inc(oT_done, 1)

            pool.sem_inc(oT_done, 1)
            G_.memset(ident[:], 1.0).then_inc(ready, 1)
            G_.memset(mask[:], 0.0).then_inc(ready, 1)
            G_.memset(nhalf[:], -0.5).then_inc(ready, 1)
            pool.wait_ge(ready, 3)
            G_.affine_select(out=ident[:], in_=ident[:], compare_op=ALU.is_equal, fill=0.0, base=0,
                             pattern=[[-1, P]], channel_multiplier=1).then_inc(consts, 1)
            G_.affine_select(out=mask[:, 384:512], in_=mask[:, 384:512], compare_op=ALU.is_ge, fill=MASKED, base=0,
                             pattern=[[-1, P]], channel_multiplier=1).then_inc(consts, 1)
            inverse_root(0)
            for fb in range(4):
                context_low(0, fb)

            def body(it):
                if not it.first:
                    expand(it, -1)
                    o_low(it, -1)
                if it.tail:
                    return
                expand(it, 0)
                o_low(it, 0)
                expand(it, 1)
                if not it.last:
                    inverse_root(it.b + 1)
                o_low(it, 1)
                if not it.last:
                    for fb in range(3):
                        context_low(it.b + 1, fb)
                expand(it, 2)
                if not it.last:
                    context_low(it.b + 1, 3)
                o_low(it, 2)
                if it.first:
                    pool.wait_ge(d_free[it.bank("B", 0)], it.bank_read("B", 0))
                pool.wait_ge(res_in, it.b * 16 + 16)
                for t in range(QT):
                    G_.tensor_tensor(out=xt[:, t, :], in0=xt[:, t, :], in1=bo_row[:],
                                     op=ALU.add).then_inc(res_ok, 1)

            over_batches(pool, body)


def stage_b(nc, x1, w1, w2, vecs, b2, out):
    B, S, D = x1.shape
    F = w1.shape[1]
    KT = D // P
    FT = F // P
    QT = S // P
    WC = F // 512
    FC = FT // WC
    RING_H = 4

    with ExitStack() as ctx:
        def sb(name, shape, dt=F32):
            return ctx.enter_context(nc.sbuf_tensor(name, shape, dt))

        def pb(name):
            return ctx.enter_context(nc.psum_tensor(name, [P, 512], F32))

        def sem(name):
            return ctx.enter_context(nc.semaphore(name))

        w1_hi = sb("w1_hi", [P, KT, F], F32R)
        w1_lo = sb("w1_lo", [P, KT, F], F32R)
        w2_hi = sb("w2_hi", [P, FT, D], F32R)
        w2_lo = sb("w2_lo", [P, FT, D], F32R)
        raw = sb("raw", [P, 2, KT, 512])
        vec = sb("vecb", [P, 2 * KT + FT])
        b1s = sb("b1s", [P, FT])
        b2_row = sb("b2_row", [P, D])
        xn = sb("xn", [P, QT, D])
        xr = sb("xr", [P, QT, D])
        hT_hi = sb("hT_hi", [P, KT, S], F32R)
        hT_lo = sb("hT_lo", [P, KT, S], F32R)
        g_sb = sb("g_sb", [P, 2, S])
        g_hi = sb("g_hi", [P, RING_H, S], F32R)
        g_lo = sb("g_lo", [P, RING_H, S], F32R)
        ident = sb("identb", [P, P])
        stats = sb("statsb", [P, QT, 6])
        mv = sb("mvb", [P, QT, 2])
        ve = sb("veb", [P, QT])
        rstd = sb("rstdb", [P, QT])
        nhalf = sb("nhalfb", [P, QT])

        bank_f = [pb(f"bank_f{i}") for i in range(2)]
        bank_x = [pb(f"bank_x{i}") for i in range(2)]
        bank_o = [pb(f"bank_o{i}") for i in range(4)]
        bank_b = [bank_o[3], bank_x[0], bank_x[0], bank_x[0]]

        carriers = sem("carriersb")
        vec_in, b2_in = sem("vecb_in"), sem("b2_in")
        raw_in = [sem(f"rawb_in{i}") for i in range(2)]
        xn_in, xr_in, stored = sem("xn_in"), sem("xr_in"), sem("out_stored")
        ready, consts, b1_mm, b1_ok, scaled = (sem(n) for n in ("readyb", "constsb", "b1_mm", "b1_ok", "scaledb"))
        w1_hi_ok, w1_ok, w2_hi_ok, w2_ok = (sem(n) for n in ("w1_hi_ok", "w1_ok", "w2_hi_ok", "w2_ok"))
        bn_ok, mv_ok, ve_ok, rstd_ok, xn_ok = (sem(n) for n in ("bnb_ok", "mvb_ok", "veb_ok", "rstdb_ok", "xnb_ok"))
        x_t, hT_hi_ok, hT_ok = (sem(n) for n in ("x_t", "hT_hi_ok", "hT_ok"))
        ffn1, gelu, g_hi_ok, g_ok, ffn2, summed, xr_ok = (
            sem(n) for n in ("ffn1", "gelu", "g_hi_ok", "g_ok", "ffn2", "summed", "xr_ok"))

        x_v = x1.rearrange("b (t p) d -> b p t d", p=P)
        out_v = out.rearrange("b (t p) d -> b p t d", p=P)
        w1_v = w1.rearrange("(t p) f -> p t f", p=P)
        w2_v = w2.rearrange("(c t p) d -> c p t d", p=P, t=FC)

        def over_chunks(eng, body):
            body(0, True, False)
            with eng.Fori(1, B - 1) as c:
                body(c, False, False)
            body(B - 1, False, True)

        block = ctx.enter_context(nc.Block())

        @block.sync
        def _(sp):
            def one(view, b):
                return view[bass.ds(b, 1)].rearrange("o p t d -> p (o t) d")

            sp.sem_inc(stored, 16)
            sp.dma_start(vec[:], vecs).then_inc(vec_in, 16)
            for wc in range(WC):
                if wc > 0:
                    sp.wait_ge(w1_ok, wc)
                sp.dma_start(raw[:, 0, :, :], w1_v[:, :, 512 * wc:512 * wc + 512]).then_inc(raw_in[0], 16)
                if wc == 0:
                    sp.dma_start(xn[:], one(x_v, 0)).then_inc(xn_in, 16)
                else:
                    sp.wait_ge(w2_ok, wc)
                sp.dma_start(raw[:, 1, :, :], w2_v[wc]).then_inc(raw_in[1], 16)
                if wc == 0:
                    sp.dma_start(b2_row[:], b2.partition_broadcast(P)).then_inc(b2_in, 16)

            def body(c, first, last):
                sp.wait_ge(stored, c * 64 + 16)
                sp.dma_start(xr[:], one(x_v, c)).then_inc(xr_in, 16)
                if not last:
                    sp.wait_ge(x_t, c * QT + QT)
                    sp.dma_start(xn[:], one(x_v, c + 1)).then_inc(xn_in, 16)
                for t in range(QT):
                    sp.wait_ge(summed, c * QT + (t + 5))
                    sp.dma_start(one(out_v, c)[:, t, :], xr[:, t, :]).then_inc(stored, 16)

            over_chunks(sp, body)
            sp.wait_ge(stored, 64 * B + 16)

        @block.tensor
        def _(pe):
            def split_product(o, lh, ll, rh, rl, first, last):
                pe.matmul(o, lh, rh, start=first, stop=False)
                pe.matmul(o, lh, rl, start=False, stop=False)
                return pe.matmul(o, ll, rh, start=False, stop=last)

            def x_transpose(m, t):
                pe.wait_ge(xn_ok, m * QT + (t + 1))
                pe.wait_ge(hT_ok, m * QT + (t + 1))
                for f in range(KT):
                    mm = pe.transpose(bank_x[t % 2][:, P * f:P * f + P], xn[:, t, P * f:P * f + P], ident[:])
                mm.then_inc(x_t, 1)

            def hidden(c, f):
                if f == 0:
                    pe.wait_ge(hT_ok, c * QT + (QT + 2))
                pe.wait_ge(gelu, c * FT + (f + 1))
                cols = slice(P * f, P * f + P)
                for kt in range(KT):
                    mm = split_product(bank_f[f % 2][:], w1_hi[:, kt, cols], w1_lo[:, kt, cols],
                                       hT_hi[:, kt, :], hT_lo[:, kt, :], kt == 0, kt == KT - 1)
                mm.then_inc(ffn1, 1)

            def output(c, f):
                pe.wait_ge(g_ok, c * FT + (f + 3))
                for t in range(QT):
                    if f == 0:
                        pe.wait_ge(summed, c * QT + (t + 1))
                    cols = slice(P * t, P * t + P)
                    mm = split_product(bank_o[t][:], g_hi[:, f % RING_H, cols], g_lo[:, f % RING_H, cols],
                                       w2_hi[:, f, :], w2_lo[:, f, :], f == 0, f == FT - 1)
                mm.then_inc(ffn2, 1)

            def bias_product(wc, bank):
                pe.wait_ge(raw_in[0], 16 * (wc + 1))
                for f in range(FC):
                    for kt in range(KT):
                        mm = pe.matmul(bank[:, f:f + 1], raw[:, 0, kt, P * f:P * f + P],
                                       vec[:, KT + kt:KT + kt + 1], start=(kt == 0), stop=(kt == KT - 1))
                mm.then_inc(b1_mm, 1)

            pe.sem_inc(ffn2, RING_H)
            pe.wait_ge(vec_in, 16)
            pe.wait_ge(consts, 1)
            bias_product(0, bank_b[0])
            for t in range(QT):
                x_transpose(0, t)

            def body(c, first, last):
                for f in range(FT):
                    wc, at = divmod(f, FC)
                    if first and at == 0:
                        pe.wait_ge(w1_ok, wc + 1)
                    if f == 0 and first:
                        pe.wait_ge(b1_ok, 1)
                    hidden(c, f)
                    if first and at == 0 and wc < WC - 1:
                        bias_product(wc + 1, bank_b[wc + 1])
                    if f >= 2:
                        if first and (f - 2) % FC == 0:
                            pe.wait_ge(w2_ok, (f - 2) // FC + 1)
                        output(c, f - 2)
                if first:
                    pe.wait_ge(b1_ok, WC)
                for half in range(2):
                    if not last:
                        x_transpose(c + 1, 2 * half)
                        x_transpose(c + 1, 2 * half + 1)
                    output(c, FT - 2 + half)

            over_chunks(pe, body)

        @block.vector
        def _(dve):
            V = nc.vector

            def layer_norm_stats(m):
                dve.wait_ge(xn_in, m * 16 + 16)
                for t in range(QT):
                    V.bn_stats(stats[:, t, :], xn[:, t, :]).then_inc(bn_ok, 1)
                for t in range(QT):
                    dve.wait_ge(bn_ok, m * QT + (t + 1))
                    dve.sem_inc(carriers, 1)
                    V.bn_aggr(mv[:, t, :], stats[:, t, :]).then_inc(mv_ok, 1)
                dve.wait_ge(mv_ok, m * QT + QT)
                V.tensor_scalar(ve[:], mv[:, :, 1], EPS, None, ALU.add).then_inc(ve_ok, 1)

            def normalise(m, t):
                if t == 0:
                    dve.wait_ge(rstd_ok, m + 1)
                V.tensor_scalar(xn[:, t, :], xn[:, t, :], mv[:, t, 0:1], rstd[:, t:t + 1],
                                ALU.subtract, ALU.mult).then_inc(xn_ok, 1)

            def x_low(m, t):
                dve.wait_ge(hT_hi_ok, m * QT + (t + 1))
                cols = slice(P * t, P * t + P)
                V.tensor_tensor(hT_lo[:, :, cols], bank_x[t % 2][:].rearrange("p (f c) -> p f c", f=KT),
                                hT_hi[:, :, cols].bitcast(F32), ALU.subtract).then_inc(hT_ok, 1)

            def split_gelu(c, f):
                dve.wait_ge(gelu, c * FT + (f + 3))
                dve.wait_ge(ffn2, c * FT + (f + 1))
                V.tensor_copy(g_hi[:, f % RING_H, :], g_sb[:, f % 2, :]).then_inc(g_hi_ok, 1)
                dve.wait_ge(g_hi_ok, c * FT + (f + 1))
                V.tensor_tensor(g_lo[:, f % RING_H, :], g_sb[:, f % 2, :], g_hi[:, f % RING_H, :].bitcast(F32),
                                ALU.subtract).then_inc(g_ok, 1)

            dve.sem_inc(hT_ok, 2)
            dve.sem_inc(g_ok, 2)
            dve.sem_inc(summed, QT)
            layer_norm_stats(0)
            dve.wait_ge(vec_in, 16)

            def scale_w1(wc):
                dve.wait_ge(b1_mm, wc + 1)
                V.tensor_tensor(b1s[:, FC * wc:FC * wc + FC], bank_b[wc][:, 0:FC],
                                vec[:, 2 * KT + FC * wc:2 * KT + FC * wc + FC], ALU.add).then_inc(b1_ok, 1)
                for kt in range(KT):
                    V.tensor_scalar(raw[:, 0, kt, :], raw[:, 0, kt, :], vec[:, kt:kt + 1], None,
                                    ALU.mult).then_inc(scaled, 1)

            def w1_low(wc):
                dve.wait_ge(w1_hi_ok, wc + 1)
                fs = slice(512 * wc, 512 * wc + 512)
                V.tensor_tensor(w1_lo[:, :, fs], raw[:, 0, :, :], w1_hi[:, :, fs].bitcast(F32),
                                ALU.subtract).then_inc(w1_ok, 1)

            scale_w1(0)
            for t in range(QT):
                normalise(0, t)
            w1_low(0)
            for t in range(QT):
                x_low(0, t)

            def body(c, first, last):
                for f in range(FT):
                    split_gelu(c, f)
                    wc, at = divmod(f, FC)
                    if first and wc < WC - 1:
                        if at == 0:
                            scale_w1(wc + 1)
                        if at == 1:
                            w1_low(wc + 1)
                    if not last:
                        start = FT - 5 if first else 2
                        if f == start:
                            layer_norm_stats(c + 1)
                        if start < f <= start + QT:
                            normalise(c + 1, f - start - 1)
                if not last:
                    for t in range(QT):
                        x_low(c + 1, t)
                dve.wait_ge(ffn2, c * FT + (FT + RING_H))
                for t in range(QT):
                    dve.wait_ge(xr_ok, c * QT + (t + 1))
                    V.tensor_tensor(xr[:, t, :], bank_o[t][:], xr[:, t, :], ALU.add).then_inc(summed, 1)

            over_chunks(dve, body)

        @block.scalar
        def _(act):
            A = nc.scalar

            def x_high(m, t):
                act.wait_ge(x_t, m * QT + (t + 1))
                A.copy(hT_hi[:, :, P * t:P * t + P],
                       bank_x[t % 2][:].rearrange("p (f c) -> p f c", f=KT)).then_inc(hT_hi_ok, 1)

            def w1_high(wc):
                act.wait_ge(scaled, KT * (wc + 1))
                A.copy(w1_hi[:, :, 512 * wc:512 * wc + 512], raw[:, 0, :, :]).then_inc(w1_hi_ok, 1)

            def w2_high(wc):
                act.wait_ge(raw_in[1], 16 * (wc + 1))
                A.copy(w2_hi[:, FC * wc:FC * wc + FC, :], raw[:, 1, :, :]).then_inc(w2_hi_ok, 1)

            act.sem_inc(gelu, 2)
            w1_high(0)
            for t in range(QT):
                x_high(0, t)
            w2_high(0)

            def body(c, first, last):
                for f in range(FT):
                    act.wait_ge(ffn1, c * FT + (f + 1))
                    if first and f % FC == 0:
                        act.wait_ge(b1_ok, f // FC + 1)
                    act.wait_ge(g_ok, c * FT + (f + 1))
                    A.activation(g_sb[:, f % 2, :], bank_f[f % 2][:], ACT.Gelu, bias=b1s[:, f:f + 1],
                                 scale=1.0).then_inc(gelu, 1)
                    wc, at = divmod(f, FC)
                    if first and wc < WC - 1:
                        if at == 1:
                            w1_high(wc + 1)
                        if at == 2:
                            w2_high(wc + 1)
                if not last:
                    for t in range(QT):
                        x_high(c + 1, t)

            over_chunks(act, body)

        @block.gpsimd
        def _(pool):
            G_ = nc.gpsimd

            def inverse_root(m):
                pool.wait_ge(ve_ok, m + 1)
                G_.tensor_tensor(out=rstd[:], in0=ve[:], in1=nhalf[:], op=ALU.pow).then_inc(rstd_ok, 1)

            G_.memset(ident[:], 1.0).then_inc(ready, 1)
            G_.memset(nhalf[:], -0.5).then_inc(ready, 1)
            pool.wait_ge(ready, 2)
            G_.affine_select(out=ident[:], in_=ident[:], compare_op=ALU.is_equal, fill=0.0, base=0,
                             pattern=[[-1, P]], channel_multiplier=1).then_inc(consts, 1)
            inverse_root(0)
            pool.wait_ge(b2_in, 16)

            def w2_low(wc):
                pool.wait_ge(w2_hi_ok, wc + 1)
                fs = slice(FC * wc, FC * wc + FC)
                G_.tensor_tensor(out=w2_lo[:, fs, :], in0=raw[:, 1, :, :], in1=w2_hi[:, fs, :].bitcast(F32),
                                 op=ALU.subtract).then_inc(w2_ok, 1)

            def body(c, first, last):
                if first:
                    for wc in range(WC):
                        w2_low(wc)
                    inverse_root(1)
                pool.wait_ge(xr_in, c * 16 + 16)
                for t in range(QT):
                    G_.tensor_tensor(out=xr[:, t, :], in0=xr[:, t, :], in1=b2_row[:], op=ALU.add).then_inc(xr_ok, 1)
                if not last and not first:
                    inverse_root(c + 1)

            over_chunks(pool, body)


def build(nc, x, ctxT, wq, wk, wv, wo, vecs_a, bo, w1, w2, vecs_b, b2, out):
    x1 = nc.dram_tensor("x1_scratch", tuple(x.shape), F32).ap()
    stage_a(nc, x, ctxT, wq, wk, wv, wo, vecs_a, bo, x1)
    stage_b(nc, x1, w1, w2, vecs_b, b2, out)


def kernel(x, ctx_1024, **w):
    import numpy as np
    import concourse.bacc as bacc
    from concourse.bass_utils import run_bass_kernel_spmd

    w = {k.replace("L0_xattn_", ""): np.asarray(v) for k, v in w.items()}
    D = x.shape[-1]

    def by_columns(v):
        return np.asarray(v).reshape(-1, P).T

    def feature_major(v):
        return v.reshape(*v.shape[:-1], HEADS // 4, 4, D // HEADS).swapaxes(-1, -2).reshape(v.shape)

    arrays = {
        "x": np.asarray(x),
        "ctxT": np.asarray(ctx_1024).transpose(0, 2, 1),
        "wq": feature_major(w["wq"]),
        "wk": feature_major(w["wk"]),
        "wv": w["wv"],
        "wo": w["wo"],
        "vecs_a": np.stack([by_columns(v) for v in (w["ln1_g"], w["ln1_b"], feature_major(w["bq"]),
                                                    feature_major(w["bk"]), w["bv"])], axis=1),
        "bo": w["bo"],
        "w1": w["w1"],
        "w2": w["w2"],
        "vecs_b": np.concatenate([by_columns(w["ln2_g"]), by_columns(w["ln2_b"]), by_columns(w["b1"])], axis=1),
        "b2": w["b2"],
    }
    nc = bacc.Bacc("TRN2", target_bir_lowering=False, num_devices=1)
    arrays = {f"in_{k}": np.ascontiguousarray(v) for k, v in arrays.items()}
    args = [nc.dram_tensor(k, v.shape, mybir.dt.from_np(v.dtype), kind="ExternalInput").ap()
            for k, v in arrays.items()]
    out = nc.dram_tensor("out", x.shape, F32, kind="ExternalOutput").ap()
    build(nc, *args, out)
    r = run_bass_kernel_spmd(nc, [arrays], core_ids=[0])
    return r.results[0]["out"]
```
